# Optimizing a Trainium2 kernel written in Bass

```python
import numpy as np
import jax
import jax.numpy as jnp

def _softmax(x, axis=-1):
    return jax.nn.softmax(x, axis=axis)

def _gelu(x):
    return jax.nn.gelu(x, approximate=True)

def _silu(x):
    return jax.nn.silu(x)

def _sigmoid(x):
    return jax.nn.sigmoid(x)

def _layernorm(x, axis=-1, eps=1e-05):
    m = jnp.mean(x, axis=axis, keepdims=True)
    v = jnp.var(x, axis=axis, keepdims=True)
    return (x - m) / jnp.sqrt(v + eps)

def _scatter_add(tgt, idx, src, axis=0):
    return tgt.at[idx].add(src)

def _segment_sum(src, seg, n):
    return jax.ops.segment_sum(src, seg, n)
kernel_name = 'mk_recurrent_d1_jaxref_r8_36e326'

def setup_inputs(seed: int=0):
    np.random.seed(seed)
    _w = jnp.asarray

    def _L0_attn_setup():
        import jax, jax.numpy as jnp
        import numpy as np
        B, T, D_IN, D = (16, 256, 128, 128)
        LN_EPS = 1e-05

        def _lru_forward(x, W_in, b_in, params_log, W_mid, b_mid, w1_w, w1_b, w2_w, w2_b, ln_g, ln_b):
            u = jnp.einsum('btd,edh->ebth', x, W_in) + b_in[:, None, None, :]
            in_r, in_i, o = (u[0], u[1], u[2])
            p = jnp.exp(params_log)
            nu, theta, gamma = (p[0], p[1], p[2])
            lam = jnp.exp(jax.lax.complex(-nu, theta))
            uc = jax.lax.complex(gamma * in_r, gamma * in_i)
            f = jnp.broadcast_to(lam, uc.shape)

            def combine(a, b):
                fa, ua = a
                fb, ub = b
                return (fa * fb, fb * ua + ub)
            _, h = jax.lax.associative_scan(combine, (f, uc), axis=1)
            hidden = jnp.concatenate([h[:, -1, :].real, h[:, -1, :].imag], axis=-1)[None]
            hri = jnp.stack([h.real, h.imag])
            out2 = jnp.einsum('ebtd,edh->ebth', hri, W_mid) + b_mid[:, None, None, :]
            out = out2[0] - out2[1] + o
            y = jax.nn.gelu(out @ w1_w + w1_b, approximate=False)
            y = y @ w2_w + w2_b + out
            mean = jnp.mean(y, axis=-1, keepdims=True)
            var = jnp.var(y, axis=-1, keepdims=True)
            y = (y - mean) * jax.lax.rsqrt(var + LN_EPS) * ln_g + ln_b
            return (y, hidden)

        def _reference_tuple_inner(x, W_in, b_in, params_log, W_mid, b_mid, w1_w, w1_b, w2_w, w2_b, ln_g, ln_b):
            return _lru_forward(x, W_in, b_in, params_log, W_mid, b_mid, w1_w, w1_b, w2_w, w2_b, ln_g, ln_b)
        key = jax.random.key(seed)
        ks = jax.random.split(key, 13)
        s_in = 1.0 / np.sqrt(D_IN)
        s_d = 1.0 / np.sqrt(D)
        x = jax.random.normal(ks[0], (B, T, D_IN), jnp.float32)
        W_in = jax.random.uniform(ks[1], (3, D_IN, D), jnp.float32, -s_in, s_in)
        b_in = jax.random.uniform(ks[2], (3, D), jnp.float32, -s_in, s_in)
        r_min, r_max = (0.9, 0.999)
        u1 = jax.random.uniform(ks[3], (D,), jnp.float32)
        u2 = jax.random.uniform(ks[4], (D,), jnp.float32)
        nu_log = jnp.log(-0.5 * jnp.log(u1 * (r_max ** 2 - r_min ** 2) + r_min ** 2))
        theta_log = jnp.log(u2 * 2.0 * np.pi)
        lam_abs = jnp.exp(-jnp.exp(nu_log))
        gamma_log = jnp.log(jnp.sqrt(1.0 - lam_abs ** 2))
        params_log = jnp.stack([nu_log, theta_log, gamma_log])
        W_mid = jax.random.uniform(ks[5], (2, D, D), jnp.float32, -s_d, s_d)
        b_mid = jax.random.uniform(ks[6], (2, D), jnp.float32, -s_d, s_d)
        w1_w = jax.random.uniform(ks[7], (D, D), jnp.float32, -s_d, s_d)
        w1_b = jax.random.uniform(ks[8], (D,), jnp.float32, -s_d, s_d)
        w2_w = jax.random.uniform(ks[9], (D, D), jnp.float32, -s_d, s_d)
        w2_b = jax.random.uniform(ks[10], (D,), jnp.float32, -s_d, s_d)
        ln_g = jnp.ones((D,), jnp.float32)
        ln_b = jnp.zeros((D,), jnp.float32)
        return {'x': x, 'W_in': W_in, 'b_in': b_in, 'params_log': params_log, 'W_mid': W_mid, 'b_mid': b_mid, 'w1_w': w1_w, 'w1_b': w1_b, 'w2_w': w2_w, 'w2_b': w2_b, 'ln_g': ln_g, 'ln_b': ln_b}
    _L0_attn_in = _L0_attn_setup()

    def _L0_ffn_setup():
        import jax, jax.numpy as jnp
        import numpy as np
        D = 128
        H = 512
        E = 8
        B, N = (2, 256)
        key = jax.random.key(seed)
        ks = jax.random.split(key, 5)
        x = jax.random.normal(ks[0], (B, N, D), dtype=jnp.float32)
        W1 = jax.random.normal(ks[1], (E, D, H), dtype=jnp.float32) / np.sqrt(D)
        W2 = jax.random.normal(ks[2], (E, H, D), dtype=jnp.float32) / np.sqrt(H)
        Wg = jax.random.normal(ks[3], (D, E), dtype=jnp.float32) / np.sqrt(D)
        bg = jax.random.normal(ks[4], (E,), dtype=jnp.float32) * 0.01
        return {'x': x, 'W1': W1, 'W2': W2, 'Wg': Wg, 'bg': bg}
    _L0_ffn_in = _L0_ffn_setup()
    _d = {'L0_attn_x': _L0_attn_in['x'], 'L0_attn_W_in': _L0_attn_in['W_in'], 'L0_attn_b_in': _L0_attn_in['b_in'], 'L0_attn_params_log': _L0_attn_in['params_log'], 'L0_attn_W_mid': _L0_attn_in['W_mid'], 'L0_attn_b_mid': _L0_attn_in['b_mid'], 'L0_attn_w1_w': _L0_attn_in['w1_w'], 'L0_attn_w1_b': _L0_attn_in['w1_b'], 'L0_attn_w2_w': _L0_attn_in['w2_w'], 'L0_attn_w2_b': _L0_attn_in['w2_b'], 'L0_attn_ln_g': _L0_attn_in['ln_g'], 'L0_attn_ln_b': _L0_attn_in['ln_b'], 'L0_ffn_W1': _L0_ffn_in['W1'], 'L0_ffn_W2': _L0_ffn_in['W2'], 'L0_ffn_Wg': _L0_ffn_in['Wg'], 'L0_ffn_bg': _L0_ffn_in['bg']}
    _x0 = _d['L0_attn_x']
    _d['L0_attn_x'] = jax.random.normal(jax.random.fold_in(jax.random.key(seed), 1), (16, 256, 128), dtype=_x0.dtype)
    del _x0
    return _d

def reference(L0_attn_x, L0_attn_W_in, L0_attn_b_in, L0_attn_params_log, L0_attn_W_mid, L0_attn_b_mid, L0_attn_w1_w, L0_attn_w1_b, L0_attn_w2_w, L0_attn_w2_b, L0_attn_ln_g, L0_attn_ln_b, L0_ffn_W1, L0_ffn_W2, L0_ffn_Wg, L0_ffn_bg):

    def _L0_attn_ref(x, W_in, b_in, params_log, W_mid, b_mid, w1_w, w1_b, w2_w, w2_b, ln_g, ln_b):
        import jax, jax.numpy as jnp
        import numpy as np
        B, T, D_IN, D = (16, 256, 128, 128)
        LN_EPS = 1e-05

        def _lru_forward(x, W_in, b_in, params_log, W_mid, b_mid, w1_w, w1_b, w2_w, w2_b, ln_g, ln_b):
            u = jnp.einsum('btd,edh->ebth', x, W_in) + b_in[:, None, None, :]
            in_r, in_i, o = (u[0], u[1], u[2])
            p = jnp.exp(params_log)
            nu, theta, gamma = (p[0], p[1], p[2])
            lam = jnp.exp(jax.lax.complex(-nu, theta))
            uc = jax.lax.complex(gamma * in_r, gamma * in_i)
            f = jnp.broadcast_to(lam, uc.shape)

            def combine(a, b):
                fa, ua = a
                fb, ub = b
                return (fa * fb, fb * ua + ub)
            _, h = jax.lax.associative_scan(combine, (f, uc), axis=1)
            hidden = jnp.concatenate([h[:, -1, :].real, h[:, -1, :].imag], axis=-1)[None]
            hri = jnp.stack([h.real, h.imag])
            out2 = jnp.einsum('ebtd,edh->ebth', hri, W_mid) + b_mid[:, None, None, :]
            out = out2[0] - out2[1] + o
            y = jax.nn.gelu(out @ w1_w + w1_b, approximate=False)
            y = y @ w2_w + w2_b + out
            mean = jnp.mean(y, axis=-1, keepdims=True)
            var = jnp.var(y, axis=-1, keepdims=True)
            y = (y - mean) * jax.lax.rsqrt(var + LN_EPS) * ln_g + ln_b
            return (y, hidden)

        def _reference_tuple_inner(x, W_in, b_in, params_log, W_mid, b_mid, w1_w, w1_b, w2_w, w2_b, ln_g, ln_b):
            return _lru_forward(x, W_in, b_in, params_log, W_mid, b_mid, w1_w, w1_b, w2_w, w2_b, ln_g, ln_b)
        return _reference_tuple_inner(x, W_in, b_in, params_log, W_mid, b_mid, w1_w, w1_b, w2_w, w2_b, ln_g, ln_b)[0]

    def _L0_ffn_ref(x, W1, W2, Wg, bg):
        import jax, jax.numpy as jnp
        import numpy as np
        D = 128
        H = 512
        E = 8
        B, N = (2, 256)
        b, n, d = x.shape
        e = Wg.shape[1]
        xf = x.reshape(b * n, d)
        logits = xf @ Wg + bg
        one_hot = jax.nn.one_hot(jnp.argmax(logits, axis=-1), e, dtype=x.dtype)
        h = jax.nn.gelu(jnp.einsum('td,edh->eth', xf, W1), approximate=True)
        y = jnp.einsum('eth,ehd->etd', h, W2)
        out = jnp.einsum('etd,te->td', y, one_hot)
        return out.reshape(b, n, d)
    x = L0_attn_x
    xn = _layernorm(x, axis=-1)
    s = _L0_attn_ref(xn, L0_attn_W_in, L0_attn_b_in, L0_attn_params_log, L0_attn_W_mid, L0_attn_b_mid, L0_attn_w1_w, L0_attn_w1_b, L0_attn_w2_w, L0_attn_w2_b, L0_attn_ln_g, L0_attn_ln_b)
    g = _silu(_L0_ffn_ref(xn, L0_ffn_W1, L0_ffn_W2, L0_ffn_Wg, L0_ffn_bg))
    x = x + s * g
    return x

_drawn_inputs = setup_inputs


def setup_inputs(seed=0):
    import zlib

    import numpy as np

    out = dict(_drawn_inputs(seed))
    spreads = {'L0_attn_ln_g': (1.0, 0.2), 'L0_attn_ln_b': (0.0, 0.1)}
    factors = {'L0_attn_w1_b': 6.279}
    for name, (base, spread) in spreads.items():
        noise = np.random.default_rng([zlib.crc32(name.encode()), seed]).standard_normal(out[name].shape)
        drawn = base * np.exp(spread * noise) if base else spread * noise
        out[name] = jnp.asarray(drawn.astype(out[name].dtype))
    for name, factor in factors.items():
        out[name] = (out[name] * factor).astype(out[name].dtype)
    return out
```

```python
from contextlib import ExitStack

import concourse.bass as bass
from concourse import mybir

P = 128
F32 = mybir.dt.float32
BF16 = mybir.dt.bfloat16
I32 = mybir.dt.int32
ALU = mybir.AluOpType
ACT = mybir.ActivationFunctionType
AX_X = mybir.AxisListType.X

CH = 4
EPS = 1e-5
TWO_PI_HI = 6.28125
TWO_PI_LO = 6.283185307179586 - TWO_PI_HI


def lru_moe(nc, x, W_small, columns, rows, W1, W2, Wg, bg, out):
    B, T, D = x.shape
    _, E, H = W1.shape
    NB = B * T // (P * CH)
    NT = NB * CH
    K = T // CH
    HALF = NB // 2
    BPH = B // 2
    HC = H // P
    NTILE = NT + E - 1
    NTOK = B * T
    RW = D + 4
    RING = 4
    NBLK = 2 * CH
    HEAD = 6
    ROUNDS = (NTILE - 1 - HEAD) // RING
    assert D == P and K * 2 == P and H == 512 and E == 8

    xs_dram = nc.dram_tensor("sorted_rows", (NTILE * P, RW), F32, kind="Internal").ap()
    gate_dram = nc.dram_tensor("gate_rows", (NTOK + RING * P, D), F32, kind="Internal").ap()

    ctx = ExitStack()
    with ctx:
        def sb(name, shape, dt=F32):
            return ctx.enter_context(nc.sbuf_tensor(name, shape, dt))

        def sem(name):
            return ctx.enter_context(nc.semaphore(name))

        bank = [ctx.enter_context(nc.psum_tensor(f"bank{i}", [P, 512], F32)) for i in range(8)]

        x_sb = sb("x_sb", [P, NB, CH, D])
        xn = sb("xn", [P, NT, RW])
        xnT = sb("xnT", [P, CH, NB * P])
        w_small = sb("w_small", [P, 7, D])
        wi, wm, w1s, w2s = w_small[:, 0:3, :], w_small[:, 3:5, :], w_small[:, 5, :], w_small[:, 6, :]
        wg = sb("wg", [P, E])
        up_w = sb("up_w", [P, E * H])
        down_w = sb("down_w", [P, E * HC * D])
        cols_sb = sb("cols_sb", [P, 10])
        plog, bin_c, bmid_c = cols_sb[:, 0:3], cols_sb[:, 3:6], cols_sb[:, 6:8]
        w1b_c, w2b_c = cols_sb[:, 8:9], cols_sb[:, 9:10]
        g_row = sb("g_row", [P, D])
        b_row = sb("b_row", [P, D])
        bg_row = sb("bg_row", [P, E])
        ident = sb("ident", [P, P])
        tri = sb("tri", [P, P], BF16)
        ones_b = sb("ones_b", [P, P], BF16)
        ones_f = sb("ones_f", [P, E * (NT + 1)])
        neg_half = sb("neg_half", [P, NT])
        e_minus = sb("e_minus", [P, E])
        tile_at = sb("tile_at", [P, NTILE])
        fill = sb("fill", [P, RING, RW])
        pexp = sb("pexp", [P, 3])
        mag = sb("mag", [P, 2])
        ang = sb("ang", [P, 8])
        angi = sb("angi", [P, 1], I32)
        cs = sb("cs", [P, 2])
        lam = sb("lam", [P, CH + 1, 2])
        glam = sb("glam", [P, CH + 1, 3])
        phas = sb("phas", [P, 16, 2])
        tmp1 = sb("tmp1", [P, 16])
        vbias = sb("vbias", [P, 2])
        cosk = sb("cosk", [P, K])
        sink = sb("sink", [P, K])
        decay = sb("decay", [P, 512])
        wT = sb("wT", [P, 2, D])
        tv = sb("tv", [P, CH - 1, 2, D])
        v_w = sb("v_w", [P, CH, 2, D])
        b_w = sb("b_w", [P, CH + 1, D])
        c_w = sb("c_w", [P, CH + 1, D])
        m_w = sb("m_w", [P, CH, D])
        wtmp = sb("wtmp", [P, 2, 5 * D])
        bm = sb("bm", [P, 1])
        obias = sb("obias", [P, CH])
        st = sb("st", [P, NT, 6])
        mv = sb("mv", [P, NT, 2])
        veps = sb("veps", [P, NT])
        rstd = sb("rstd", [P, NT])
        lg = sb("lg", [P, NT, E])
        cand = sb("cand", [P, NT, E])
        top = sb("top", [P, NT])
        pick = sb("pick", [P, NT])
        onehot = sb("onehot", [P, E, NT], BF16)
        totals = sb("totals", [P, E, NT])
        cnt = sb("cnt", [P, E])
        cnti = sb("cnti", [P, E], I32)
        aug = sb("aug", [P, E, NT + 1])
        base = sb("base", [P, E, NT + 1])
        posm = sb("posm", [P, E, NT])
        slot_f = sb("slot_f", [P, NT])
        slot = sb("slot", [P, NT], I32)
        tcmp = sb("tcmp", [P, NTILE, E - 1])
        tex_f = sb("tex_f", [P, NTILE])
        tex = sb("tex", [P, NTILE], I32)
        ra = sb("ra", [P, 512])
        rb = sb("rb", [P, 512])
        rc = sb("rc", [P, 512])
        rd = sb("rd", [P, 512])
        gs = sb("gs", [P, 2, 512])
        carry = sb("carry", [P, 2, NB * P])
        outT = sb("outT", [P, 4, 512])
        g1 = sb("g1", [P, 2, 512])
        yT = sb("yT", [P, 2, 512])
        fst = sb("fst", [P, NT, 6])
        fmv = sb("fmv", [P, NT, 2])
        fveps = sb("fveps", [P, NT])
        frstd = sb("frstd", [P, NT])
        s_sb = sb("s_sb", [P, NB, CH, D])
        xs_in = sb("xs_in", [P, RING, RW])
        xsT = sb("xsT", [P, 2, P])
        hid = sb("hid", [P, 2, H])
        hidT = sb("hidT", [P, 2, H])
        th = sb("th", [P, 2, D])
        gate = sb("gate", [P, RING, D])
        token = sb("token", [P, NTILE], I32)
        gate_in = sb("gate_in", [P, NB, CH, D])

        x_in = [sem(f"x_in{i}") for i in range(NB)]
        par_in = sem("par_in")
        win_in = sem("win_in")
        wmid_in = sem("wmid_in")
        row_in = sem("row_in")
        up_in = sem("up_in")
        down_in = sem("down_in")
        const_ready = sem("const_ready")
        pool_step = sem("pool_step")
        dve_step = sem("dve_step")
        act_step = sem("act_step")
        fill_ready = sem("fill_ready")
        filled = sem("filled")
        exp_ready = sem("exp_ready")
        ang_ready = sem("ang_ready")
        cs_ready = sem("cs_ready")
        wT_done = sem("wT_done")
        wT_ready = sem("wT_ready")
        tv_ready = sem("tv_ready")
        vT_done = sem("vT_done")
        v_ready = sem("v_ready")
        bc_ready = sem("bc_ready")
        m_done = sem("m_done")
        m_ready = sem("m_ready")
        stat_ready = sem("stat_ready")
        rstd_ready = sem("rstd_ready")
        xn_ready = sem("xn_ready")
        xT_done = sem("xT_done")
        xT_ready = sem("xT_ready")
        logits_done = sem("logits_done")
        onehot_ready = sem("onehot_ready")
        count_done = sem("count_done")
        slot_ready = sem("slot_ready")
        tex_ready = sem("tex_ready")
        vin_done = sem("vin_done")
        carry_ready = sem("carry_ready")
        o_done = sem("o_done")
        outT_ready = sem("outT_ready")
        w1_done = sem("w1_done")
        g1_ready = sem("g1_ready")
        w2_done = sem("w2_done")
        y_ready = sem("y_ready")
        yT_done = sem("yT_done")
        fstat_ready = sem("fstat_ready")
        frstd_ready = sem("frstd_ready")
        z_ready = sem("z_ready")
        s_ready = sem("s_ready")
        sorted_out = sem("sorted_out")
        xs_ld = [sem(f"xs_ld{i}") for i in range(RING)]
        xsT_done = sem("xsT_done")
        xsT_ready = sem("xsT_ready")
        up_done = sem("up_done")
        hid_ready = sem("hid_ready")
        hidT_done = sem("hidT_done")
        hidT_ready = sem("hidT_ready")
        down_done = sem("down_done")
        th_ready = sem("th_ready")
        gate_ready = sem("gate_ready")
        gate_out = [sem(f"gate_out{i}") for i in range(RING)]
        gate_ld = [sem(f"gate_ld{i}") for i in range(NB)]
        prod_ready = sem("prod_ready")
        sum_ready = sem("sum_ready")
        stored = sem("stored")

        ps_wT = bank[4]
        ps_vT = [bank[5], bank[6]]
        ps_x = [bank[0], bank[1]]
        ps_lg = bank[2]
        ps_rt = bank[3]
        ps_v = [[bank[4], bank[5]], [bank[6], bank[7]]]
        ps_m, ps_mb = bank[0], bank[1]
        ps_o = [bank[0], bank[1]]
        ps_1 = [bank[2], bank[3]]
        ps_2 = [bank[6], bank[7]]
        ps_y = [bank[4], bank[5]]
        ps_xs = [bank[0], bank[7]]
        ps_up = [bank[1], bank[2]]
        ps_hT = [bank[3], bank[4]]
        ps_dn = [bank[5], bank[6]]

        x_dram = x.rearrange("b t d -> (b t) d").rearrange("(g p j) d -> g p j d", p=P, j=CH)
        out_dram = out.rearrange("b t d -> (b t) d").rearrange("(g p j) d -> g p j d", p=P, j=CH)
        gate_v = gate_dram[0:NTOK, :].rearrange("(g p j) d -> g p j d", p=P, j=CH)

        def tok(bb, j):
            return xnT[:, j, bb * P:(bb + 1) * P]

        def bk(ap):
            return ap.rearrange("p (b k) -> p b k", k=K)

        def over_b(tab, n=K):
            return tab.unsqueeze(1).broadcast_to([P, BPH, n])

        block = ctx.enter_context(nc.Block())

        @block.sync
        def _(sp):
            for bb in range(NB):
                sp.dma_start(x_sb[:, bb, :, :], x_dram[bb]).then_inc(x_in[bb], 16)
            sp.wait_ge(fill_ready, 1)
            rounds = NTILE // RING
            whole = rounds * RING * P
            for u in range(RING):
                sp.dma_start(xs_dram[0:whole, :].rearrange("(i u p) c -> u p i c", u=RING, p=P)[u],
                             fill[:, u, :].unsqueeze(1).broadcast_to([P, rounds, RW])).then_inc(filled, 16)
            sp.dma_start(xs_dram[whole:NTILE * P, :].rearrange("(u p) c -> p u c", p=P),
                         fill[:, 0:NTILE - rounds * RING, :]).then_inc(filled, 16)
            sp.dma_start(up_w[:, :], W1.rearrange("d e h -> d (e h)")).then_inc(up_in, 16)
            sp.dma_start(down_w[:, :], W2.rearrange("p e c d -> p (e c d)")).then_inc(down_in, 16)

            sp.wait_ge(sorted_out, 16 * NT)

            def load(t, r):
                sp.dma_start(xs_in[:, r, :], xs_dram[bass.ds(t * P, P), :]).then_inc(xs_ld[r], 16)

            for t in range(RING):
                load(t, t)
            rounds = NTILE // RING - 1
            with sp.Fori(0, rounds) as i:
                for u in range(RING):
                    sp.wait_ge(xsT_ready, i * RING + u + 1)
                    load(i * RING + u + RING, u)
            for t in range((rounds + 1) * RING, NTILE):
                sp.wait_ge(xsT_ready, t - RING + 1)
                load(t, t % RING)

            for r in range(RING):
                sp.wait_ge(gate_out[r], 16 * ((NTILE - r + RING - 1) // RING))
            for bb in range(NB):
                sp.dma_start(gate_in[:, bb, :, :], gate_v[bb]).then_inc(gate_ld[bb], 16)
            for bb in range(NB):
                sp.wait_ge(sum_ready, bb + 1)
                sp.dma_start(out_dram[bb], x_sb[:, bb, :, :]).then_inc(stored, 16)
            sp.wait_ge(stored, 16 * NB)

        @block.gpsimd
        def _(pool):
            count = [0]

            def link(ins):
                count[0] += 1
                ins.then_inc(pool_step, 1)
                pool.wait_ge(pool_step, count[0])

            nc.gpsimd.memset(neg_half[:], -0.5)
            nc.gpsimd.memset(tri[:], 1.0)
            nc.gpsimd.memset(ones_b[:], 1.0)
            nc.gpsimd.memset(ones_f[:], 1.0)
            nc.gpsimd.memset(fill[:], 0.0)
            nc.gpsimd.memset(carry[:], 0.0)
            link(nc.gpsimd.memset(ident[:], 0.0))
            nc.gpsimd.affine_select(out=ident[:], in_=ident[:], compare_op=ALU.not_equal, fill=1.0,
                                    base=0, pattern=[[1, P]], channel_multiplier=-1)
            nc.gpsimd.affine_select(out=tri[:], in_=tri[:], compare_op=ALU.is_gt, fill=0.0,
                                    base=0, pattern=[[1, P]], channel_multiplier=-1)
            nc.gpsimd.iota(e_minus[:], pattern=[[1, E]], base=-E, channel_multiplier=0,
                           allow_small_or_imprecise_dtypes=True)
            nc.gpsimd.iota(tile_at[:], pattern=[[P, NTILE]], base=0, channel_multiplier=0,
                           allow_small_or_imprecise_dtypes=True)
            nc.gpsimd.iota(xn[:, :, D:RW].bitcast(I32), pattern=[[P * CH, NB], [1, CH], [0, RW - D]],
                           base=0, channel_multiplier=CH).then_inc(const_ready, 1)
            nc.gpsimd.iota(fill[:, :, D:RW].bitcast(I32), pattern=[[P, RING], [0, RW - D]],
                           base=NTOK, channel_multiplier=1).then_inc(fill_ready, 1)
            for bb in range(NB):
                n = slice(bb * CH, (bb + 1) * CH)
                pool.wait_ge(stat_ready, bb + 1)
                link(nc.gpsimd.tensor_scalar(veps[:, n], mv[:, n, 1], EPS, None, ALU.add))
                nc.gpsimd.tensor_tensor(rstd[:, n], veps[:, n], neg_half[:, n], ALU.pow).then_inc(rstd_ready, 1)
            pool.wait_ge(filled, 16 * (RING + 1))
            pool.wait_ge(slot_ready, 1)
            for n in range(NT):
                nc.gpsimd.indirect_dma_start(out=xs_dram, out_offset=bass.IndirectOffsetOnAxis(ap=slot[:, n:n + 1], axis=0),
                                             in_=xn[:, n, :], in_offset=None).then_inc(sorted_out, 16)
            def affine(b):
                hf, j = divmod(b, CH)
                z = s_sb[:, hf * HALF:(hf + 1) * HALF, j, :]
                pool.wait_ge(z_ready, b + 1)
                link(nc.gpsimd.tensor_tensor(z, z, g_row[:].unsqueeze(1).broadcast_to([P, HALF, D]), ALU.mult))
                nc.gpsimd.tensor_tensor(z, z, b_row[:].unsqueeze(1).broadcast_to([P, HALF, D]),
                                        ALU.add).then_inc(s_ready, 1)

            pool.wait_ge(row_in, 16 * 3)
            link(nc.gpsimd.tensor_scalar(g_row[:], g_row[:], 0.5, None, ALU.mult))
            link(nc.gpsimd.tensor_scalar(b_row[:], b_row[:], 0.5, None, ALU.mult))
            for b in range(NBLK):
                pool.wait_ge(fstat_ready, b + 1)
                n = slice(b * HALF, (b + 1) * HALF)
                link(nc.gpsimd.tensor_scalar(fveps[:, n], fmv[:, n, 1], EPS, None, ALU.add))
                nc.gpsimd.tensor_tensor(frstd[:, n], fveps[:, n], neg_half[:, n], ALU.pow).then_inc(frstd_ready, 1)
                if b >= 1:
                    affine(b - 1)
            affine(NBLK - 1)
            for t in range(NTILE):
                pool.wait_ge(gate_ready, t + 1)
                nc.gpsimd.indirect_dma_start(out=gate_dram, out_offset=bass.IndirectOffsetOnAxis(ap=token[:, t:t + 1], axis=0),
                                             in_=gate[:, t % RING, :], in_offset=None).then_inc(gate_out[t % RING], 16)
            for bb in range(NB):
                pool.wait_ge(prod_ready, bb + 1)
                nc.gpsimd.tensor_tensor(x_sb[:, bb, :, :], x_sb[:, bb, :, :], gate_in[:, bb, :, :],
                                        ALU.add).then_inc(sum_ready, 1)

        @block.scalar
        def _(act):
            act.dma_start(cols_sb[:, :], columns).then_inc(par_in, 16)
            act.dma_start(w_small[:, 0:3, :], W_small[:, 0:3, :]).then_inc(win_in, 16)
            act.dma_start(wg[:, :], Wg).then_inc(win_in, 16)
            act.dma_start(w_small[:, 3:7, :], W_small[:, 3:7, :]).then_inc(wmid_in, 16)
            act.dma_start(bg_row[:, :], bg.rearrange("(a d) -> a d", a=1).broadcast_to([P, E])).then_inc(row_in, 16)
            act.dma_start(g_row[:, :], rows[0:1, :].broadcast_to([P, D])).then_inc(row_in, 16)
            act.dma_start(b_row[:, :], rows[1:2, :].broadcast_to([P, D])).then_inc(row_in, 16)

            act.wait_ge(par_in, 16)
            nc.scalar.activation(pexp[:], plog, ACT.Exp).then_inc(act_step, 1)
            act.wait_ge(act_step, 1)
            nc.scalar.activation(mag[:, 0:1], pexp[:, 0:1], ACT.Exp, scale=-1.0)
            nc.scalar.activation(mag[:, 1:2], pexp[:, 0:1], ACT.Exp, scale=-float(CH)).then_inc(exp_ready, 1)
            act.wait_ge(ang_ready, 1)
            nc.scalar.activation(cs[:], ang[:, 4:6], ACT.Sin).then_inc(cs_ready, 1)
            act.wait_ge(wT_done, 1)
            nc.scalar.copy(wT[:, :, :], ps_wT[:, 0:2 * D]).then_inc(wT_ready, 1)

            def evac_x(bb):
                act.wait_ge(xT_done, bb + 1)
                nc.scalar.copy(xnT[:, :, bb * P:(bb + 1) * P],
                               ps_x[bb % 2][:, :].rearrange("p (j c) -> p j c", j=CH)).then_inc(xT_ready, 1)

            for bb in range(NB):
                evac_x(bb)
            act.wait_ge(vT_done, 1)
            nc.scalar.copy(v_w[:, 1:3, :, :], ps_vT[0][:, :])
            nc.scalar.copy(v_w[:, 3, :, :], ps_vT[1][:, 0:2 * D]).then_inc(v_ready, 1)

            for b in range(NBLK + 1):
                if b < NBLK:
                    act.wait_ge(o_done, b + 1)
                    if b >= 4:
                        act.wait_ge(y_ready, b - 3)
                    nc.scalar.activation(outT[:, b % 4, :], ps_o[b % 2][:, :], ACT.Identity,
                                         bias=obias[:, b % CH:b % CH + 1]).then_inc(outT_ready, 1)
                if b >= 1:
                    k = b - 1
                    act.wait_ge(w1_done, k + 1)
                    if k >= 2:
                        act.wait_ge(w2_done, k - 1)
                    nc.scalar.activation(g1[:, k % 2, :], ps_1[k % 2][:, :], ACT.Gelu,
                                         bias=w1b_c[:, 0:1]).then_inc(g1_ready, 1)

            def hidden(t, s):
                r2 = s % 2
                act.wait_ge(up_done, t + 1)
                if s >= 2:
                    act.wait_ge(hidT_done, t - 1)
                nc.scalar.activation(hid[:, r2, :], ps_up[r2][:, :], ACT.Gelu_apprx_tanh).then_inc(hid_ready, 1)

            def tanh(t, s):
                r2 = s % 2
                act.wait_ge(down_done, t + 1)
                nc.scalar.activation(th[:, r2, :], ps_dn[r2][:, 0:D], ACT.Tanh, scale=0.5).then_inc(th_ready, 1)

            def step(t, s):
                if s < NTILE:
                    hidden(t, s)
                if s >= 2:
                    tanh(t - 2, s - 2)

            for t in range(HEAD):
                step(t, t)
            with act.Fori(0, ROUNDS) as i:
                for u in range(RING):
                    step(i * RING + HEAD + u, HEAD + u)
            for t in range(HEAD + ROUNDS * RING, NTILE + 2):
                step(t, t)

        @block.vector
        def _(dve):
            count = [0]

            def mark(ins):
                count[0] += 1
                ins.then_inc(dve_step, 1)

            def settle():
                dve.wait_ge(dve_step, count[0])

            def link(ins):
                mark(ins)
                settle()

            V = nc.vector
            pl, ql = lambda l: lam[:, l, 0:1], lambda l: lam[:, l, 1:2]

            def cmul(dst, a, b):
                mark(V.tensor_tensor(tmp1[:, 0:2], a, b, ALU.mult))
                mark(V.tensor_tensor(tmp1[:, 2:3], a[:, 0:1], b[:, 1:2], ALU.mult))
                link(V.tensor_tensor(tmp1[:, 3:4], a[:, 1:2], b[:, 0:1], ALU.mult))
                mark(V.tensor_tensor(dst[:, 0:1], tmp1[:, 0:1], tmp1[:, 1:2], ALU.subtract))
                link(V.tensor_tensor(dst[:, 1:2], tmp1[:, 2:3], tmp1[:, 3:4], ALU.add))

            dve.wait_ge(exp_ready, 1)
            link(V.tensor_scalar(ang[:, 0:1], pexp[:, 1:2], 1.0 / 6.283185307179586, None, ALU.mult))
            link(V.tensor_copy(angi[:], ang[:, 0:1]))
            link(V.tensor_copy(ang[:, 1:2], angi[:]))
            link(V.scalar_tensor_tensor(out=ang[:, 2:3], in0=ang[:, 1:2], scalar=-TWO_PI_HI, in1=pexp[:, 1:2],
                                        op0=ALU.mult, op1=ALU.add))
            link(V.scalar_tensor_tensor(out=ang[:, 3:4], in0=ang[:, 1:2], scalar=-TWO_PI_LO, in1=ang[:, 2:3],
                                        op0=ALU.mult, op1=ALU.add))
            link(V.tensor_scalar(ang[:, 4:5], ang[:, 3:4], 3.1415925, -3.1415925, ALU.min, ALU.max))
            link(V.tensor_scalar(ang[:, 6:7], ang[:, 4:5], -1.0, None, ALU.mult))
            link(V.tensor_tensor(ang[:, 7:8], ang[:, 4:5], ang[:, 6:7], ALU.max))
            V.tensor_scalar(ang[:, 5:6], ang[:, 7:8], -1.0, 1.5707963267948966,
                            ALU.mult, ALU.add).then_inc(ang_ready, 1)

            def stats(bb):
                dve.wait_ge(x_in[bb], 16)
                for j in range(CH):
                    mark(V.bn_stats(st[:, bb * CH + j, :], x_sb[:, bb, j, :]))
                settle()
                for j in range(CH):
                    last = V.bn_aggr(mv[:, bb * CH + j, :], st[:, bb * CH + j, :])
                last.then_inc(stat_ready, 1)

            def normalise(bb):
                dve.wait_ge(rstd_ready, bb + 1)
                for j in range(CH):
                    n = bb * CH + j
                    last = V.tensor_scalar(xn[:, n, 0:D], x_sb[:, bb, j, :], mv[:, n, 0:1], rstd[:, n:n + 1],
                                           ALU.subtract, ALU.mult)
                last.then_inc(xn_ready, 1)

            stats(0)
            for bb in range(1, NB):
                stats(bb)
                normalise(bb - 1)
            normalise(NB - 1)

            dve.wait_ge(cs_ready, 1)
            mark(V.memset(lam[:, 0, 0:1], 1.0))
            mark(V.memset(lam[:, 0, 1:2], 0.0))
            mark(V.tensor_scalar(pl(1), cs[:, 1:2], mag[:, 0:1], None, ALU.mult))
            mark(V.tensor_scalar(ql(1), cs[:, 0:1], mag[:, 0:1], None, ALU.mult))
            mark(V.tensor_copy(phas[:, 8, 0:1], cs[:, 1:2]))
            link(V.tensor_copy(phas[:, 8, 1:2], cs[:, 0:1]))
            for l in range(1, CH):
                cmul(lam[:, l + 1, :], lam[:, l, :], lam[:, 1, :])
            dve.wait_ge(wT_ready, 1)
            for l in range(1, CH):
                mark(V.tensor_scalar(wtmp[:, 0, l * D:(l + 1) * D], wT[:, 1, :], ql(l), None, ALU.mult))
                link(V.tensor_scalar(wtmp[:, 1, l * D:(l + 1) * D], wT[:, 1, :], pl(l), None, ALU.mult))
                V.scalar_tensor_tensor(out=tv[:, l - 1, 0, :], in0=wT[:, 0, :], scalar=pl(l),
                                       in1=wtmp[:, 0, l * D:(l + 1) * D], op0=ALU.mult, op1=ALU.subtract)
                last = V.scalar_tensor_tensor(out=tv[:, l - 1, 1, :], in0=wT[:, 0, :], scalar=ql(l),
                                              in1=wtmp[:, 1, l * D:(l + 1) * D], op0=ALU.mult, op1=ALU.add)
            last.then_inc(tv_ready, 1)

            dve.wait_ge(logits_done, 1)
            dve.wait_ge(row_in, 16 * 3)
            dve.wait_ge(const_ready, 1)
            link(V.tensor_tensor(lg[:], ps_lg[:, 0:NT * E].rearrange("p (n e) -> p n e", e=E),
                                 bg_row[:].unsqueeze(1).broadcast_to([P, NT, E]), ALU.add))
            link(V.tensor_reduce(top[:], lg[:], AX_X, ALU.max))
            link(V.tensor_tensor(cand[:], lg[:], top[:].unsqueeze(2).broadcast_to([P, NT, E]), ALU.is_equal))
            link(V.tensor_tensor(cand[:], cand[:], e_minus[:].unsqueeze(1).broadcast_to([P, NT, E]), ALU.mult))
            link(V.tensor_reduce(pick[:], cand[:], AX_X, ALU.min))
            V.tensor_tensor(onehot[:], pick[:].unsqueeze(1).broadcast_to([P, E, NT]),
                            e_minus[:].unsqueeze(2).broadcast_to([P, E, NT]), ALU.is_equal).then_inc(onehot_ready, 1)
            dve.wait_ge(count_done, 1)
            before = ps_rt[:, 0:E * NT].rearrange("p (e n) -> p e n", e=E)
            mark(V.tensor_copy(aug[:, :, 1:NT + 1], ps_rt[:, E * NT:2 * E * NT].rearrange("p (e n) -> p e n", e=E)))
            settle()
            link(V.tensor_reduce(cnt[:], aug[:, :, 1:NT + 1], AX_X, ALU.add))
            link(V.tensor_scalar(cnti[:], cnt[:], float(P - 1), None, ALU.add))
            link(V.tensor_scalar(cnti[:], cnti[:], 7, 7, ALU.logical_shift_right, ALU.logical_shift_left))
            mark(V.memset(aug[:, 0, 0:1], 0.0))
            link(V.tensor_tensor(aug[:, 1:E, 0], cnti[:, 0:E - 1], cnt[:, 0:E - 1], ALU.subtract))
            link(V.tensor_tensor_scan(base[:].rearrange("p e n -> p (e n)"), ones_f[:],
                                      aug[:].rearrange("p e n -> p (e n)"), 0.0, ALU.mult, ALU.add))
            link(V.tensor_tensor(posm[:], before, base[:, :, 0:NT], ALU.add))
            link(V.tensor_tensor(posm[:], posm[:], onehot[:], ALU.mult))
            link(V.tensor_reduce(slot_f[:], posm[:].rearrange("p e n -> p n e"), AX_X, ALU.add))
            V.tensor_copy(slot[:], slot_f[:]).then_inc(slot_ready, 1)
            link(V.tensor_tensor(tcmp[:], tile_at[:].unsqueeze(2).broadcast_to([P, NTILE, E - 1]),
                                 base[:, 1:E, 0].unsqueeze(1).broadcast_to([P, NTILE, E - 1]), ALU.is_ge))
            link(V.tensor_reduce(tex_f[:], tcmp[:], AX_X, ALU.add))
            V.tensor_scalar(tex[:], tex_f[:], float(H), None, ALU.mult).then_inc(tex_ready, 1)

            link(V.tensor_reduce(tmp1[:, 4:6], lam[:, 0:CH, :].rearrange("p l c -> p c l"), AX_X, ALU.add))
            cmul(vbias[:, 0:2], bin_c[:, 0:2], tmp1[:, 4:6])
            cmul(phas[:, 9, :], phas[:, 8, :], phas[:, 8, :])
            cmul(phas[:, 0, :], phas[:, 9, :], phas[:, 9, :])
            mark(V.memset(cosk[:, 0:1], 1.0))
            link(V.memset(sink[:, 0:1], 0.0))
            n, s = 1, 0
            while n < K:
                c_n, s_n = phas[:, s, 0:1], phas[:, s, 1:2]
                mark(V.tensor_scalar(ra[:, 0:n], sink[:, 0:n], s_n, None, ALU.mult))
                link(V.tensor_scalar(rb[:, 0:n], sink[:, 0:n], c_n, None, ALU.mult))
                mark(V.scalar_tensor_tensor(out=sink[:, n:2 * n], in0=cosk[:, 0:n], scalar=s_n, in1=rb[:, 0:n],
                                            op0=ALU.mult, op1=ALU.add))
                link(V.scalar_tensor_tensor(out=cosk[:, n:2 * n], in0=cosk[:, 0:n], scalar=c_n, in1=ra[:, 0:n],
                                            op0=ALU.mult, op1=ALU.subtract))
                if 2 * n < K:
                    cmul(phas[:, s + 1, :], phas[:, s, :], phas[:, s, :])
                n, s = 2 * n, s + 1
            link(V.tensor_scalar(decay[:], ones_f[:, 0:1].broadcast_to([P, 512]), mag[:, 1:2], None, ALU.mult))
            link(V.memset(bk(decay[:])[:, :, 0:1], 0.0))

            dve.wait_ge(wmid_in, 16)
            mark(V.tensor_scalar(glam[:, :, 0:2], lam[:, :, :], pexp[:, 2:3], None, ALU.mult))
            settle()
            link(V.tensor_scalar(glam[:, :, 2:3], glam[:, :, 1:2], -1.0, None, ALU.mult))
            for l in range(CH + 1):
                mark(V.tensor_scalar(wtmp[:, 0, l * D:(l + 1) * D], wm[:, 1, :], glam[:, l, 1:2], None, ALU.mult))
                mark(V.tensor_scalar(wtmp[:, 1, l * D:(l + 1) * D], wm[:, 1, :], glam[:, l, 0:1], None, ALU.mult))
            settle()
            for l in range(CH + 1):
                V.scalar_tensor_tensor(out=b_w[:, l, :], in0=wm[:, 0, :], scalar=glam[:, l, 0:1],
                                       in1=wtmp[:, 0, l * D:(l + 1) * D], op0=ALU.mult, op1=ALU.subtract)
                last = V.scalar_tensor_tensor(out=c_w[:, l, :], in0=wm[:, 0, :], scalar=glam[:, l, 2:3],
                                              in1=wtmp[:, 1, l * D:(l + 1) * D], op0=ALU.mult, op1=ALU.subtract)
            last.then_inc(bc_ready, 1)
            link(V.tensor_tensor(bm[:], bmid_c[:, 0:1], bmid_c[:, 1:2], ALU.subtract))
            link(V.tensor_tensor(bm[:], bm[:], bin_c[:, 2:3], ALU.add))

            def recurrence(hf):
                vr, vi = ps_v[hf][0], ps_v[hf][1]
                br, bi = vbias[:, 0:1], vbias[:, 1:2]
                dve.wait_ge(vin_done, hf + 1)
                if hf:
                    dve.wait_ge(carry_ready, hf)
                for dst, src, b, tab in ((ra, vr, br, cosk), (rb, vi, bi, sink), (rc, vi, bi, cosk), (rd, vr, br, sink)):
                    mark(V.scalar_tensor_tensor(out=bk(dst[:]), in0=bk(src[:]), scalar=b, in1=over_b(tab[:]),
                                                op0=ALU.add, op1=ALU.mult))
                settle()
                mark(V.tensor_tensor(ra[:], ra[:], rb[:], ALU.add))
                mark(V.tensor_tensor(rc[:], rc[:], rd[:], ALU.subtract))
                settle()
                mark(V.tensor_tensor_scan(gs[:, 0, :], decay[:], ra[:], 0.0, ALU.mult, ALU.add))
                link(V.tensor_tensor_scan(gs[:, 1, :], decay[:], rc[:], 0.0, ALU.mult, ALU.add))
                for dst, c, tab in ((ra, 0, cosk), (rb, 1, sink), (rc, 0, sink), (rd, 1, cosk)):
                    mark(V.tensor_tensor(bk(dst[:]), bk(gs[:, c, :]), over_b(tab[:]), ALU.mult))
                settle()
                cols = slice(hf * 512, (hf + 1) * 512)
                V.tensor_tensor(bk(carry[:, 0, cols])[:, :, 1:K], bk(ra[:])[:, :, 0:K - 1],
                                bk(rb[:])[:, :, 0:K - 1], ALU.subtract)
                last = V.tensor_tensor(bk(carry[:, 1, cols])[:, :, 1:K], bk(rc[:])[:, :, 0:K - 1],
                                       bk(rd[:])[:, :, 0:K - 1], ALU.add)
                last.then_inc(carry_ready, 1)

            recurrence(0)
            dve.wait_ge(m_done, 1)
            V.tensor_tensor(m_w[:, 0, :], ps_m[:, 0:D], wi[:, 2, :], ALU.add)
            V.tensor_copy(m_w[:, 1:CH, :], ps_m[:, D:CH * D])
            V.tensor_tensor_scan(obias[:], ones_f[:, 0:CH], ps_mb[:, 0:CH], bm[:, 0:1],
                                 ALU.mult, ALU.add).then_inc(m_ready, 1)
            recurrence(1)

            for b in range(2, NBLK + 4):
                k = b - 2
                if k < NBLK:
                    dve.wait_ge(w2_done, k + 1)
                    if k >= 2:
                        dve.wait_ge(yT_done, k - 1)
                    V.scalar_tensor_tensor(out=yT[:, k % 2, :], in0=ps_2[k % 2][:, :], scalar=w2b_c[:, 0:1],
                                           in1=outT[:, k % 4, :], op0=ALU.add, op1=ALU.add).then_inc(y_ready, 1)
                k = b - 4
                if k >= 0:
                    hf, j = divmod(k, CH)
                    dve.wait_ge(frstd_ready, k + 1)
                    for q in range(HALF):
                        n = k * HALF + q
                        last = V.tensor_scalar(s_sb[:, hf * HALF + q, j, :], ps_y[k % 2][:, q * P:(q + 1) * P],
                                               fmv[:, n, 0:1], frstd[:, n:n + 1], ALU.subtract, ALU.mult)
                    last.then_inc(z_ready, 1)
                k = b - 3
                if 0 <= k < NBLK:
                    dve.wait_ge(yT_done, k + 1)
                    for q in range(HALF):
                        mark(V.bn_stats(fst[:, k * HALF + q, :], ps_y[k % 2][:, q * P:(q + 1) * P]))
                    settle()
                    for q in range(HALF):
                        last = V.bn_aggr(fmv[:, k * HALF + q, :], fst[:, k * HALF + q, :])
                    last.then_inc(fstat_ready, 1)

            def evac_x(t, s):
                dve.wait_ge(xsT_done, t + 1)
                V.tensor_copy(token[:, bass.ds(t, 1)], xs_in[:, s % RING, D:D + 1].bitcast(I32))
                V.tensor_copy(xsT[:, s % 2, :], ps_xs[s % 2][:, 0:P]).then_inc(xsT_ready, 1)

            def evac_h(t, s):
                r2 = s % 2
                dve.wait_ge(hidT_done, t + 1)
                V.tensor_copy(hidT[:, r2, :], ps_hT[r2][:, :]).then_inc(hidT_ready, 1)

            def silu2(t, s, rnd):
                dve.wait_ge(th_ready, t + 1)
                if s >= RING:
                    dve.wait_ge(gate_out[s % RING], rnd * 16)
                V.scalar_tensor_tensor(out=gate[:, s % RING, :], in0=th[:, s % 2, :], scalar=1.0,
                                       in1=ps_dn[s % 2][:, 0:D], op0=ALU.add, op1=ALU.mult).then_inc(gate_ready, 1)

            def step(t, s, rnd):
                if s + 1 < NTILE:
                    evac_x(t + 1, s + 1)
                if 0 <= s - 1 < NTILE:
                    evac_h(t - 1, s - 1)
                if s >= 2:
                    silu2(t - 2, s - 2, rnd)

            evac_x(0, 0)
            for t in range(HEAD):
                step(t, t, (t - 2) // RING)
            with dve.Fori(0, ROUNDS) as i:
                for u in range(RING):
                    step(i * RING + HEAD + u, HEAD + u, i + (HEAD + u - 2) // RING)
            for t in range(HEAD + ROUNDS * RING, NTILE + 2):
                step(t, t, (t - 2) // RING)

            for bb in range(NB):
                dve.wait_ge(gate_ld[bb], 16)
                dve.wait_ge(s_ready, NBLK)
                V.tensor_tensor(gate_in[:, bb, :, :], gate_in[:, bb, :, :], s_sb[:, bb, :, :],
                                ALU.mult).then_inc(prod_ready, 1)

        @block.tensor
        def _(pe):
            mm, tr = nc.tensor.matmul, nc.tensor.transpose
            pe.wait_ge(const_ready, 1)
            pe.wait_ge(win_in, 16 * 2)
            tr(ps_wT[:, 0:D], wi[:, 0, :], ident[:])
            tr(ps_wT[:, D:2 * D], wi[:, 1, :], ident[:]).then_inc(wT_done, 1)

            def logits(bb):
                pe.wait_ge(xT_ready, bb + 1)
                for j in range(CH):
                    n = bb * CH + j
                    last = mm(ps_lg[:, n * E:(n + 1) * E], tok(bb, j), wg[:], start=True, stop=True)
                return last

            for bb in range(NB):
                pe.wait_ge(xn_ready, bb + 1)
                for j in range(CH):
                    last = tr(ps_x[bb % 2][:, j * P:(j + 1) * P], xn[:, bb * CH + j, 0:D], ident[:])
                last.then_inc(xT_done, 1)
                if bb >= 1:
                    logits(bb - 1)
            logits(NB - 1).then_inc(logits_done, 1)

            pe.wait_ge(tv_ready, 1)
            for i in range(2 * (CH - 1)):
                l, c = divmod(i, 2)
                last = tr(ps_vT[i // 4][:, (i % 4) * D:(i % 4 + 1) * D], tv[:, l, c, :], ident[:])
            last.then_inc(vT_done, 1)

            pe.wait_ge(onehot_ready, 1)
            hot = onehot[:].rearrange("p e n -> p (e n)")
            mm(ps_rt[:, 0:E * NT], tri[:], hot, start=True, stop=True)
            mm(ps_rt[:, E * NT:2 * E * NT], ones_b[:], hot, start=True, stop=True).then_inc(count_done, 1)

            pe.wait_ge(v_ready, 1)
            for hf in range(2):
                for c in range(2):
                    for i in range(CH):
                        w = wi[:, c, :] if i == CH - 1 else v_w[:, CH - 1 - i, c, :]
                        last = mm(ps_v[hf][c][:, :], w, xnT[:, i, hf * 512:(hf + 1) * 512],
                                  start=(i == 0), stop=(i == CH - 1))
                last.then_inc(vin_done, 1)

            pe.wait_ge(bc_ready, 1)
            pe.wait_ge(wT_ready, 1)
            mm(ps_m[:, :], wT[:, 0, :], b_w[:, 0:CH, :].rearrange("p l d -> p (l d)"), start=True, stop=False)
            mm(ps_m[:, :], wT[:, 1, :], c_w[:, 0:CH, :].rearrange("p l d -> p (l d)"), start=False, stop=True)
            for l in range(CH):
                mm(ps_mb[:, l:l + 1], b_w[:, l, :], bin_c[:, 0:1], start=True, stop=False)
                last = mm(ps_mb[:, l:l + 1], c_w[:, l, :], bin_c[:, 1:2], start=False, stop=True)
            last.then_inc(m_done, 1)
            pe.wait_ge(m_ready, 1)

            def out_block(b):
                hf, j = divmod(b, CH)
                cols = slice(hf * 512, (hf + 1) * 512)
                if b >= 2:
                    pe.wait_ge(outT_ready, b - 1)
                for i in range(j + 1):
                    mm(ps_o[b % 2][:, :], m_w[:, j - i, :], xnT[:, i, cols], start=(i == 0), stop=False)
                pe.wait_ge(carry_ready, hf + 1)
                mm(ps_o[b % 2][:, :], b_w[:, j + 1, :], carry[:, 0, cols], start=False, stop=False)
                mm(ps_o[b % 2][:, :], c_w[:, j + 1, :], carry[:, 1, cols], start=False, stop=True).then_inc(o_done, 1)

            for b in range(NBLK + 3):
                if b < NBLK:
                    out_block(b)
                k = b - 1
                if 0 <= k < NBLK:
                    pe.wait_ge(outT_ready, k + 1)
                    mm(ps_1[k % 2][:, :], w1s, outT[:, k % 4, :], start=True, stop=True).then_inc(w1_done, 1)
                k = b - 2
                if 0 <= k < NBLK:
                    pe.wait_ge(g1_ready, k + 1)
                    if k < 2:
                        pe.wait_ge(carry_ready, 2)
                    else:
                        pe.wait_ge(y_ready, k - 1)
                    mm(ps_2[k % 2][:, :], w2s, g1[:, k % 2, :], start=True, stop=True).then_inc(w2_done, 1)
                k = b - 3
                if 0 <= k < NBLK:
                    pe.wait_ge(y_ready, k + 1)
                    if k >= 2:
                        pe.wait_ge(z_ready, k - 1)
                    for q in range(HALF):
                        last = tr(ps_y[k % 2][:, q * P:(q + 1) * P], yT[:, k % 2, q * P:(q + 1) * P], ident[:])
                    last.then_inc(yT_done, 1)

            pe.wait_ge(tex_ready, 1)
            pe.wait_ge(up_in, 16)
            pe.wait_ge(down_in, 16)
            pe.wait_ge(outT_ready, NBLK)
            pe.wait_ge(g1_ready, NBLK)
            pe.wait_ge(z_ready, NBLK)

            def transpose_x(t, s, rnd):
                r = s % RING
                pe.wait_ge(xs_ld[r], rnd * 16 + 16)
                tr(ps_xs[s % 2][:, 0:P], xs_in[:, r, 0:D], ident[:]).then_inc(xsT_done, 1)

            def expert(t):
                return pe.value_load(tex[0:1, bass.ds(t, 1)], min_val=0, max_val=(E - 1) * H)

            def up(t, s):
                e = expert(t)
                pe.wait_ge(xsT_ready, t + 1)
                mm(ps_up[s % 2][:, :], xsT[:, s % 2, :], up_w[:, bass.ds(e, H)], start=True, stop=True).then_inc(up_done, 1)

            def transpose_h(t, s):
                pe.wait_ge(hid_ready, t + 1)
                for c in range(HC):
                    last = tr(ps_hT[s % 2][:, c * P:(c + 1) * P], hid[:, s % 2, c * P:(c + 1) * P], ident[:])
                last.then_inc(hidT_done, 1)

            def down(t, s):
                e = expert(t)
                pe.wait_ge(hidT_ready, t + 1)
                if s >= 2:
                    pe.wait_ge(gate_ready, t - 1)
                for c in range(HC):
                    last = mm(ps_dn[s % 2][:, 0:D], hidT[:, s % 2, c * P:(c + 1) * P],
                              down_w[:, bass.ds(e + c * D, D)], start=(c == 0), stop=(c == HC - 1))
                last.then_inc(down_done, 1)

            def step(t, s, rnd):
                if s + 1 < NTILE:
                    transpose_x(t + 1, s + 1, rnd)
                if s < NTILE:
                    up(t, s)
                if 0 <= s - 1 < NTILE:
                    transpose_h(t - 1, s - 1)
                if s >= 2:
                    down(t - 2, s - 2)

            transpose_x(0, 0, 0)
            for t in range(HEAD):
                step(t, t, (t + 1) // RING)
            with pe.Fori(0, ROUNDS) as i:
                for u in range(RING):
                    step(i * RING + HEAD + u, HEAD + u, i + (HEAD + u + 1) // RING)
            for t in range(HEAD + ROUNDS * RING, NTILE + 2):
                step(t, t, (t + 1) // RING)


def kernel(L0_attn_x, L0_attn_W_in, L0_attn_b_in, L0_attn_params_log, L0_attn_W_mid, L0_attn_b_mid,
           L0_attn_w1_w, L0_attn_w1_b, L0_attn_w2_w, L0_attn_w2_b, L0_attn_ln_g, L0_attn_ln_b,
           L0_ffn_W1, L0_ffn_W2, L0_ffn_Wg, L0_ffn_bg):
    import numpy as np
    import concourse.bacc as bacc
    from concourse.bass_utils import run_bass_kernel_spmd

    E, H, D = L0_ffn_W2.shape
    laid_out = {
        "x": L0_attn_x,
        "w_small": np.concatenate([L0_attn_W_in, L0_attn_W_mid, L0_attn_w1_w[None], L0_attn_w2_w[None]]
                                  ).transpose(1, 0, 2),
        "columns": np.concatenate([L0_attn_params_log, L0_attn_b_in, L0_attn_b_mid, L0_attn_w1_b[None],
                                   L0_attn_w2_b[None]]).transpose(1, 0),
        "rows": np.stack([L0_attn_ln_g, L0_attn_ln_b]),
        "w1": np.asarray(L0_ffn_W1).transpose(1, 0, 2),
        "w2": np.asarray(L0_ffn_W2).reshape(E, H // P, P, D).transpose(2, 0, 1, 3),
        "wg": L0_ffn_Wg,
        "bg": L0_ffn_bg,
    }
    nc = bacc.Bacc("TRN2", target_bir_lowering=False, num_devices=1)
    arrays, args = {}, []
    for name, value in laid_out.items():
        a = np.ascontiguousarray(value)
        arrays[f"{name}_dram"] = a
        args.append(nc.dram_tensor(f"{name}_dram", a.shape, mybir.dt.from_np(a.dtype), kind="ExternalInput").ap())
    out = nc.dram_tensor("out_dram", L0_attn_x.shape, F32, kind="ExternalOutput").ap()
    lru_moe(nc, *args, out)
    r = run_bass_kernel_spmd(nc, [arrays], core_ids=[0])
    return r.results[0]["out_dram"]
```

```python
from contextlib import ExitStack

import concourse.bass as bass
from concourse import mybir

P = 128
F32 = mybir.dt.float32
F32R = mybir.dt.float32r
BF16 = mybir.dt.bfloat16
I32 = mybir.dt.int32
ALU = mybir.AluOpType
ACT = mybir.ActivationFunctionType
AX_X = mybir.AxisListType.X

CH = 4
EPS = 1e-5
TWO_PI = 6.283185307179586
TWO_PI_HI = 6.28125
TWO_PI_LO = TWO_PI - TWO_PI_HI


def lru_moe(nc, x, W_small, columns, rows, W1, W2, Wg, bg, out):
    B, T, D = x.shape
    _, E, H = W1.shape
    NB = B * T // (P * CH)
    NT = NB * CH
    K = T // CH
    HALF = NB // 2
    BPH = B // 2
    COLS = BPH * K
    HC = H // P
    NTILE = NT + E - 1
    NTOK = B * T
    RW = D + 4
    RING = 4
    NBLK = 2 * CH
    HEAD = 10
    ROUNDS = (NTILE - 2 - HEAD) // RING
    NWORD = -(-NTILE // RING)
    WCH = H
    NWCH = E * H // WCH
    UP_DMA = 4
    ACT_J = CH - 1
    WARM = 8
    XB = 4
    PAIRS = NB // 2
    assert D == P and K * 2 == P and H == 512 and E == 8 and NB == 8 and HEAD % RING == 2

    xs_dram = nc.dram_tensor("sorted_rows", (NTILE * P, RW), F32, kind="Internal").ap()
    gate_dram = nc.dram_tensor("gate_rows", (NTOK + RING * P, D), F32, kind="Internal").ap()

    ctx = ExitStack()
    with ctx:
        def sb(name, shape, dt=F32):
            return ctx.enter_context(nc.sbuf_tensor(name, shape, dt))

        def sem(name):
            return ctx.enter_context(nc.semaphore(name))

        bank = [ctx.enter_context(nc.psum_tensor(f"bank{i}", [P, 512], F32)) for i in range(8)]

        x_sb = sb("x_sb", [P, NB, CH, D])
        xn = sb("xn", [P, NT, RW])
        x_h = sb("x_h", [P, CH, NB * P], F32R)
        x_l = sb("x_l", [P, CH, NB * P], F32R)
        w_small = sb("w_small", [P, 7, D])
        wi, wm, w1s, w2s = w_small[:, 0:3, :], w_small[:, 3:5, :], w_small[:, 5, :], w_small[:, 6, :]
        wg = sb("wg", [P, E])
        wg_hl = sb("wg_hl", [P, 2 * E], F32R)
        wg_h, wg_l = wg_hl[:, 0:E], wg_hl[:, E:2 * E]
        up_h = sb("up_h", [P, E * H], F32R)
        up_l = sb("up_l", [P, E * H], F32R)
        down_w = sb("down_w", [P, E * H])
        cols_sb = sb("cols_sb", [P, 10])
        plog, bin_c, bmid_c = cols_sb[:, 0:3], cols_sb[:, 3:6], cols_sb[:, 6:8]
        w1b_c, w2b_c = cols_sb[:, 8:9], cols_sb[:, 9:10]
        g_row = sb("g_row", [P, D])
        b_row = sb("b_row", [P, D])
        bg_row = sb("bg_row", [P, E])
        ident = sb("ident", [P, P])
        tri = sb("tri", [P, P], BF16)
        ones_b = sb("ones_b", [P, P], BF16)
        neg_half = sb("neg_half", [P, HALF])
        eps_c = sb("eps_c", [P, 1])
        e_minus = sb("e_minus", [P, E])
        tile_at = sb("tile_at", [P, NTILE])
        pexp = sb("pexp", [P, 3])
        mag = sb("mag", [P, 2])
        ang = sb("ang", [P, 6])
        angi = sb("angi", [P, 1], I32)
        pw = sb("pw", [P, 3, 2, CH + 1])
        glam = sb("glam", [P, 3, CH + 1])
        lamb = sb("lamb", [P, 2, CH])
        lamt = sb("lamt", [P, 2, 2, CH])
        gw = sb("gw", [P, 2, D])
        tab = sb("tab", [P, 3, K + 1])
        cosk, sink = tab[:, 1, 0:K], tab[:, 2, 0:K]
        pwt = sb("pwt", [P, 2, 2, 2 * (CH + 1)])
        vbias = sb("vbias", [P, 2])
        decay = sb("decay", [P, COLS])
        wT = sb("wT", [P, 2, D])
        b_w = sb("b_w", [P, CH, D])
        c_w = sb("c_w", [P, CH, D])
        m_h = sb("m_h", [P, CH, D], F32R)
        m_l = sb("m_l", [P, CH, D], F32R)
        bm = sb("bm", [P, 1])
        obias = sb("obias", [P, CH])
        st = sb("st", [P, NT, 6])
        mv = sb("mv", [P, NT, 2])
        std = sb("std", [P, NT])
        rstd = sb("rstd", [P, NT])
        nmr = sb("nmr", [P, NT])
        fst = sb("fst", [P, NT, 6])
        fmv = sb("fmv", [P, NT, 2])
        fveps = sb("fveps", [P, NT])
        fnmean = sb("fnmean", [P, NT])
        frstd = sb("frstd", [P, NT])
        fnmr = sb("fnmr", [P, NT])
        top = sb("top", [P, NT])
        pick = sb("pick", [P, NT])
        cnt = sb("cnt", [P, E])
        cnti = sb("cnti", [P, E], I32)
        slot_f = sb("slot_f", [P, NT])
        slot = sb("slot", [P, NT], I32)
        tex_f = sb("tex_f", [P, NWORD + 1, RING])
        tex_r = sb("tex_r", [P, NWORD + 1, 1])
        tex = sb("tex", [P, NWORD], I32)
        eights = sb("eights", [P, RING])
        token = sb("token", [P, NTILE], I32)
        rot = sb("rot", [P, 4, COLS])
        ra, rb, rc, rd = rot[:, 0, :], rot[:, 1, :], rot[:, 2, :], rot[:, 3, :]
        tabt = rot[:, 0, 0:4 * (K // 2 + 1)].rearrange("p (a b k) -> p a b k", a=2, b=2)
        ones_f = rot[:, 3, 0:E * (NT + 1)]
        carry = sb("carry", [P, 2, NB * P])
        s_sb = sb("s_sb", [P, NB, CH, D])
        fill = sb("fill", [P, RING, RW])
        v_h = sb("v_h", [P, CH, 2, D], F32R)
        v_l = sb("v_l", [P, CH, 2, D], F32R)
        xs_in = sb("xs_in", [P, RING, RW])
        xs_h = sb("xs_h", [P, 2, P], F32R)
        xs_l = sb("xs_l", [P, 2, P], F32R)
        ht = sb("ht", [P, 2, H])
        th = sb("th", [P, 2, D])
        gate = sb("gate", [P, RING, D])
        blk = sb("blk", [P, 8, COLS])
        outT, g1, yT = blk[:, 0:4, :], blk[:, 4:6, :], blk[:, 6:8, :]
        hid = blk[:, 0:2, :]
        early = blk[:, :, :].rearrange("p a b -> p (a b)")

        def part(at, *shape):
            n = 1
            for d in shape:
                n *= d
            names = " ".join("abc"[:len(shape)])
            return early[:, at:at + n].rearrange(f"p ({names}) -> p {names}", **dict(zip("abc", shape)))

        tv = part(0, CH - 1, 2, D)
        tvp = part(768, CH - 1, 2, D)
        wtmp = part(1536, 2, CH, D)
        lg = part(2816, NT, E)
        posm = part(2816, E, NT)
        cand = part(3072, NT, E)
        aug = part(3328, E, NT + 1)
        base = part(3592, E, NT + 1)
        onehot = early[:, 3856:3856 + E * NT // 2].bitcast(BF16).rearrange("p (e n) -> p e n", e=E)
        tcmp = part(768, NTILE, E - 1)
        m_0 = part(0, D)[:, :]

        x_in = [sem(f"x_in{i}") for i in range(NB)]
        par_in = sem("par_in")
        win_in = sem("win_in")
        wmid_in = sem("wmid_in")
        row_in = sem("row_in")
        up_in = [sem(f"up_in{i}") for i in range(UP_DMA)]
        down_in = sem("down_in")
        wH_ready = sem("wH_ready")
        wL_ready = sem("wL_ready")
        const_ready = sem("const_ready")
        pool_step = sem("pool_step")
        dve_step = sem("dve_step")
        act_step = sem("act_step")
        fill_ready = sem("fill_ready")
        eps_ready = sem("eps_ready")
        filled = sem("filled")
        wgH_ready = sem("wgH_ready")
        wgL_ready = sem("wgL_ready")
        exp_ready = sem("exp_ready")
        ang_ready = sem("ang_ready")
        cs_ready = sem("cs_ready")
        lam_ready = sem("lam_ready")
        table_ready = sem("table_ready")
        decay_ready = sem("decay_ready")
        wT_done = sem("wT_done")
        wT_ready = sem("wT_ready")
        tvp_ready = sem("tvp_ready")
        tv_ready = sem("tv_ready")
        vT_done = sem("vT_done")
        vH_ready = sem("vH_ready")
        vL_ready = sem("vL_ready")
        wtmp_ready = sem("wtmp_ready")
        bc_ready = sem("bc_ready")
        gw_ready = sem("gw_ready")
        m_done = sem("m_done")
        m0_ready = sem("m0_ready")
        mH_ready = sem("mH_ready")
        mL_ready = sem("mL_ready")
        stat_ready = sem("stat_ready")
        rstd_ready = sem("rstd_ready")
        xn_ready = sem("xn_ready")
        xnp_ready = sem("xnp_ready")
        std_ready = sem("std_ready")
        xT_done = sem("xT_done")
        xH_ready = sem("xH_ready")
        xL_ready = sem("xL_ready")
        logits_done = sem("logits_done")
        onehot_ready = sem("onehot_ready")
        count_done = sem("count_done")
        slot_ready = sem("slot_ready")
        tex_ready = sem("tex_ready")
        vin_done = sem("vin_done")
        rot_ready = sem("rot_ready")
        carry_ready = sem("carry_ready")
        o_done = sem("o_done")
        outT_ready = sem("outT_ready")
        w1_done = sem("w1_done")
        g1_ready = sem("g1_ready")
        w2_done = sem("w2_done")
        y_ready = sem("y_ready")
        yT_done = sem("yT_done")
        ytok_ready = sem("ytok_ready")
        fstat_ready = sem("fstat_ready")
        frstd_ready = sem("frstd_ready")
        row_ready = sem("row_ready")
        sorted_out = sem("sorted_out")
        xs_ld = [sem(f"xs_ld{i}") for i in range(RING)]
        xsT_done = sem("xsT_done")
        xsH_ready = sem("xsH_ready")
        xsL_ready = sem("xsL_ready")
        up_done = sem("up_done")
        hid_ready = sem("hid_ready")
        hT_done = sem("hT_done")
        ht_ready = sem("ht_ready")
        down_done = sem("down_done")
        th_ready = sem("th_ready")
        gate_ready = sem("gate_ready")
        gate_out = [sem(f"gate_out{i}") for i in range(RING)]
        gate_ld = [sem(f"gate_ld{i}") for i in range(NB)]
        sn_ready = sem("sn_ready")
        half0_ready = sem("half0_ready")
        half1_ready = sem("half1_ready")
        stored = sem("stored")

        ps_wT = bank[4]
        ps_vT = [bank[4], bank[6]]
        ps_x = [bank[0], bank[1], bank[7], bank[5]]
        ps_lg = bank[2]
        ps_rt = bank[3]
        ps_v = [[bank[4], bank[5]], [bank[6], bank[7]]]
        ps_m, ps_mb = bank[0], bank[1]
        ps_o = [bank[0], bank[1]]
        ps_1 = [bank[2], bank[3]]
        ps_2 = [bank[6], bank[7]]
        ps_y = [bank[4], bank[5]]
        ps_xs = [bank[0], bank[2]]
        ps_up = [bank[1], bank[3]]
        ps_hT = [bank[6], bank[7]]
        ps_dn = [bank[4], bank[5]]

        x_dram = x.rearrange("b t d -> (b t) d").rearrange("(g p j) d -> g p j d", p=P, j=CH)
        out_dram = out.rearrange("b t d -> (b t) d").rearrange("(g p j) d -> g p j d", p=P, j=CH)
        gate_v = gate_dram[0:NTOK, :].rearrange("(g p j) d -> g p j d", p=P, j=CH)
        gate_in = xn[:, :, 0:D].rearrange("p (g j) d -> p g j d", j=CH)
        up_dram, down_dram = W1.rearrange("d e h -> d (e h)"), W2.rearrange("p e c d -> p (e c d)")

        def bk(ap):
            return ap.rearrange("p (b k) -> p b k", k=K)

        def over_b(tab):
            return tab.unsqueeze(1).broadcast_to([P, BPH, K])

        def s_blk(b):
            hf, j = divmod(b, CH)
            return s_sb[:, hf * HALF:(hf + 1) * HALF, j, :]

        def q3(ap):
            return ap.rearrange("p (q d) -> p q d", d=D)

        block = ctx.enter_context(nc.Block())

        @block.sync
        def _(sp):
            for bb in range(NB):
                sp.dma_start(x_sb[:, bb, :, :], x_dram[bb]).then_inc(x_in[bb], 16)
                if bb == 1:
                    sp.dma_start(wg[:, :], Wg).then_inc(win_in, 16)
            sp.dma_start(w_small[:, 3:7, :], W_small[:, 3:7, :]).then_inc(wmid_in, 16)
            sp.dma_start(bg_row[:, :], bg.rearrange("(a d) -> a d", a=1).broadcast_to([P, E])).then_inc(row_in, 16)
            sp.dma_start(g_row[:, :], rows[0:1, :].broadcast_to([P, D])).then_inc(row_in, 16)
            sp.dma_start(b_row[:, :], rows[1:2, :].broadcast_to([P, D])).then_inc(row_in, 16)
            sp.wait_ge(fill_ready, 1)
            rounds = NTILE // RING
            whole = rounds * RING * P
            for u in range(RING):
                sp.dma_start(xs_dram[0:whole, :].rearrange("(i u p) c -> u p i c", u=RING, p=P)[u],
                             fill[:, u, :].unsqueeze(1).broadcast_to([P, rounds, RW])).then_inc(filled, 16)
            sp.dma_start(xs_dram[whole:NTILE * P, :].rearrange("(u p) c -> p u c", p=P),
                         fill[:, 0:NTILE - rounds * RING, :]).then_inc(filled, 16)
            for i in range(UP_DMA):
                cols = slice(i * E * H // UP_DMA, (i + 1) * E * H // UP_DMA)
                sp.dma_start(up_l[:, cols].bitcast(F32), up_dram[:, cols]).then_inc(up_in[i], 16)
            sp.dma_start(down_w[:, :], down_dram).then_inc(down_in, 16)

            sp.wait_ge(sorted_out, 16 * NT)

            def load(t, r):
                sp.dma_start(xs_in[:, r, :], xs_dram[bass.ds(t * P, P), :]).then_inc(xs_ld[r], 16)

            for t in range(RING):
                load(t, t)
            rounds = NTILE // RING - 1
            with sp.Fori(0, rounds) as i:
                for u in range(RING):
                    sp.wait_ge(xsL_ready, i * RING + u + 1)
                    load(i * RING + u + RING, u)
            for t in range((rounds + 1) * RING, NTILE):
                sp.wait_ge(xsL_ready, t - RING + 1)
                load(t, t % RING)

            for r in range(RING):
                sp.wait_ge(gate_out[r], 16 * ((NTILE - r + RING - 1) // RING))
            for bb in [*range(HALF, NB), *range(HALF)]:
                sp.dma_start(gate_in[:, bb, :, :], gate_v[bb]).then_inc(gate_ld[bb], 16)
            for bb in range(HALF):
                sp.wait_ge(half0_ready, bb + 1)
                sp.dma_start(out_dram[bb], x_sb[:, bb, :, :]).then_inc(stored, 16)
            for j in range(CH):
                sp.wait_ge(half1_ready, j + 1)
                sp.dma_start(out_dram[HALF:NB, :, j, :].rearrange("g p d -> p g d"),
                             x_sb[:, HALF:NB, j, :]).then_inc(stored, 16)
            sp.wait_ge(stored, 16 * (HALF + CH))

        @block.gpsimd
        def _(pool):
            G = nc.gpsimd
            count = [0]

            def mark(ins):
                count[0] += 1
                ins.then_inc(pool_step, 1)

            def link(ins):
                mark(ins)
                pool.wait_ge(pool_step, count[0])

            mark(G.memset(ident[:], 0.0))
            mark(G.memset(tri[:], 1.0))
            mark(G.memset(fill[:], 0.0))
            G.memset(neg_half[:], -0.5)
            mark(G.memset(pw[:, :, :, 0:1], 0.0))
            mark(G.memset(tab[:, :, 0:1], 0.0))
            G.memset(eps_c[:], EPS).then_inc(eps_ready, 1)
            for i in range(RING):
                G.memset(eights[:, i:i + 1], float(E ** i))
            mark(G.memset(tex_f[:], 0.0))
            G.memset(ones_b[:], 1.0)
            link(G.memset(ones_f, 1.0))
            G.affine_select(out=ident[:], in_=ident[:], compare_op=ALU.not_equal, fill=1.0,
                            base=0, pattern=[[1, P]], channel_multiplier=-1)
            G.affine_select(out=tri[:], in_=tri[:], compare_op=ALU.is_gt, fill=0.0,
                            base=0, pattern=[[1, P]], channel_multiplier=-1)
            G.iota(e_minus[:], pattern=[[1, E]], base=-E, channel_multiplier=0,
                   allow_small_or_imprecise_dtypes=True)
            G.iota(tile_at[:], pattern=[[P, NTILE]], base=0, channel_multiplier=0,
                   allow_small_or_imprecise_dtypes=True)
            G.iota(fill[:, :, D:RW].bitcast(I32), pattern=[[P, RING], [0, RW - D]],
                   base=NTOK, channel_multiplier=1).then_inc(fill_ready, 1)
            G.iota(xn[:, :, D:RW].bitcast(I32), pattern=[[P * CH, NB], [1, CH], [0, RW - D]],
                   base=0, channel_multiplier=CH).then_inc(const_ready, 1)

            mark(G.memset(pw[:, 1, :, 0:1], 1.0))
            mark(G.memset(tab[:, 1, 0:1], 1.0))

            def normalise(bb):
                pool.wait_ge(rstd_ready, bb // 2 + 1)
                for j in range(ACT_J, CH):
                    n = bb * CH + j
                    last = G.tensor_scalar(xn[:, n, 0:D], x_sb[:, bb, j, :], mv[:, n, 0:1], rstd[:, n:n + 1],
                                           ALU.subtract, ALU.mult)
                last.then_inc(xnp_ready, 1)

            def extend(powers, tmp, n):
                shape = list(powers[:, 1:3, ..., 0:n + 1].shape)
                re = powers[:, 1:2, ..., n:n + 1].broadcast_to(shape)
                im = powers[:, 2:3, ..., n:n + 1].broadcast_to(shape)
                a, b = tmp
                mark(G.tensor_tensor(a, powers[:, 1:3, ..., 0:n + 1], re, ALU.mult))
                link(G.tensor_tensor(b, powers[:, 0:2, ..., 0:n + 1], im, ALU.mult))
                link(G.tensor_tensor(powers[:, 1:3, ..., n:2 * n + 1], a, b, ALU.add))
                link(G.tensor_scalar(powers[:, 0, ..., n:2 * n + 1], powers[:, 2, ..., n:2 * n + 1], -1.0, None,
                                     ALU.mult))

            def extend_pw(n):
                extend(pw, [pwt[:, i, :, 0:2 * (n + 1)].rearrange("p a (c l) -> p a c l", c=2) for i in range(2)], n)

            pool.wait_ge(cs_ready, 1)
            link(G.tensor_scalar(pw[:, 1:3, 1, 1], pw[:, 1:3, 0, 1], mag[:, 0:1], None, ALU.mult))
            link(G.tensor_scalar(pw[:, 0, :, 1], pw[:, 2, :, 1], -1.0, None, ALU.mult))
            extend_pw(1)
            normalise(0)
            extend_pw(2)
            normalise(1)
            G.tensor_scalar(glam[:, :, :], pw[:, :, 1, :], pexp[:, 2:3], None, ALU.mult).then_inc(lam_ready, 1)
            normalise(2)
            pool.wait_ge(wT_ready, 1)
            for l in range(1, CH):
                G.tensor_scalar(tvp[:, l - 1, 0, :], wT[:, 1, :], pw[:, 2, 1, l:l + 1], None, ALU.mult)
                last = G.tensor_scalar(tvp[:, l - 1, 1, :], wT[:, 1, :], pw[:, 1, 1, l:l + 1], None, ALU.mult)
                if l == CH - 1:
                    last.then_inc(tvp_ready, 1)
                normalise(l + 2)
            for bb in range(CH + 2, NB):
                normalise(bb)
            pool.wait_ge(wmid_in, 16)
            G.tensor_scalar(gw[:, 0, :], wm[:, 0, :], pexp[:, 2:3], None, ALU.mult)
            mark(G.tensor_scalar(gw[:, 1, :], wm[:, 1, :], pexp[:, 2:3], -1.0, ALU.mult, ALU.mult))
            mark(G.tensor_scalar(lamt[:, 0, :, :], pw[:, 1:3, 1, 0:CH], bin_c[:, 0:1], None, ALU.mult))
            link(G.tensor_scalar(lamt[:, 1, :, :], pw[:, 0:2, 1, 0:CH], bin_c[:, 1:2], None, ALU.mult))
            mark(G.tensor_tensor(lamb[:, :, :], lamt[:, 0, :, :], lamt[:, 1, :, :], ALU.add))
            pool.wait_ge(pool_step, count[0])
            G.tensor_tensor(lamt[:, 0, :, 0:2], lamb[:, :, 0:2], lamb[:, :, 2:4], ALU.add).then_inc(gw_ready, 1)
            pool.wait_ge(gw_ready, 1)
            mark(G.tensor_tensor(vbias[:, 0:2], lamt[:, 0, :, 0], lamt[:, 0, :, 1], ALU.add))
            link(G.tensor_copy(tab[:, :, 1], pw[:, :, 0, CH]))
            n = 1
            while n < K:
                extend(tab, [tabt[:, i, :, 0:n + 1] for i in range(2)], n)
                n *= 2
            mark(G.memset(carry[:, :, :].rearrange("p c (b k) -> p (c b) k", k=K)[:, :, 0:1], 0.0))
            pool.wait_ge(decay_ready, 1)
            mark(G.memset(bk(decay[:])[:, :, 0:1], 0.0))
            link(G.tensor_tensor(bm[:], bmid_c[:, 0:1], bmid_c[:, 1:2], ALU.subtract))
            G.tensor_tensor(bm[:], bm[:], bin_c[:, 2:3], ALU.add).then_inc(table_ready, 1)

            pool.wait_ge(filled, 16 * (RING + 1))
            pool.wait_ge(slot_ready, 1)
            for n in range(NT):
                G.indirect_dma_start(out=xs_dram, out_offset=bass.IndirectOffsetOnAxis(ap=slot[:, n:n + 1], axis=0),
                                     in_=xn[:, n, :], in_offset=None).then_inc(sorted_out, 16)

            def inverse_std(b, done):
                n = slice(b * HALF, (b + 1) * HALF)
                mark(G.tensor_scalar(fveps[:, n], fmv[:, n, 1], EPS, None, ALU.add))
                link(G.tensor_scalar(fnmean[:, n], fmv[:, n, 0], -1.0, None, ALU.mult))
                link(G.tensor_tensor(frstd[:, n], fveps[:, n], neg_half[:], ALU.pow))
                G.tensor_tensor(fnmr[:, n], fnmean[:, n], frstd[:, n], ALU.mult).then_inc(done, 1)

            def normalise_s(j):
                pool.wait_ge(frstd_ready, j + 1)
                for q in range(HALF):
                    n = j * HALF + q
                    mark(G.tensor_scalar(s_sb[:, q, j, :], s_sb[:, q, j, :], frstd[:, n:n + 1], fnmr[:, n:n + 1],
                                         ALU.mult, ALU.add))

            def affine(j, row, op):
                pool.wait_ge(pool_step, count[0])
                mark(G.tensor_tensor(s_blk(j), s_blk(j),
                                     row[:].unsqueeze(1).broadcast_to([P, HALF, D]), op))

            pool.wait_ge(row_ready, 2)
            for t in range(NTILE):
                pool.wait_ge(gate_ready, t + 1)
                G.indirect_dma_start(out=gate_dram, out_offset=bass.IndirectOffsetOnAxis(ap=token[:, t:t + 1], axis=0),
                                     in_=gate[:, t % RING, :], in_offset=None).then_inc(gate_out[t % RING], 16)
                if t < CH:
                    pool.wait_ge(fstat_ready, t + 1)
                    inverse_std(t, frstd_ready)
                j, stage_of = divmod(t - 4, 8)
                if 0 <= t - 4 and j < CH:
                    if stage_of == 0:
                        normalise_s(j)
                    elif stage_of == 3:
                        affine(j, g_row, ALU.mult)
                    elif stage_of == 6:
                        affine(j, b_row, ALU.add)

            def combine(bb):
                pool.wait_ge(gate_ld[bb], 16)
                link(G.tensor_tensor(s_sb[:, bb, :, :], s_sb[:, bb, :, :], gate_in[:, bb, :, :], ALU.mult))
                G.tensor_tensor(x_sb[:, bb, :, :], x_sb[:, bb, :, :], s_sb[:, bb, :, :],
                                ALU.add).then_inc(half0_ready, 1)

            pool.wait_ge(pool_step, count[0])
            for bb in range(HALF):
                combine(bb)
            for k in range(CH, NBLK):
                pool.wait_ge(fstat_ready, k + 1)
                inverse_std(k, frstd_ready)

        @block.scalar
        def _(act):
            S = nc.scalar
            act.dma_start(cols_sb[:, :], columns).then_inc(par_in, 16)
            act.dma_start(w_small[:, 0:3, :], W_small[:, 0:3, :]).then_inc(win_in, 16)

            act.wait_ge(par_in, 16)
            S.activation(pexp[:], plog, ACT.Exp).then_inc(act_step, 1)
            act.wait_ge(act_step, 1)
            S.activation(mag[:, 0:1], pexp[:, 0:1], ACT.Exp, scale=-1.0)
            S.activation(mag[:, 1:2], pexp[:, 0:1], ACT.Exp, scale=-float(CH)).then_inc(exp_ready, 1)
            act.wait_ge(win_in, 32)
            S.copy(wg_h, wg[:]).then_inc(wgH_ready, 1)
            act.wait_ge(wT_done, 1)
            S.copy(wT[:, :, :], ps_wT[:, 0:2 * D]).then_inc(wT_ready, 1)

            act.wait_ge(ang_ready, 1)
            S.activation(pw[:, 1:3, 0, 1], ang[:, 4:6], ACT.Sin).then_inc(cs_ready, 1)

            def deviation(pair):
                act.wait_ge(stat_ready, 2 * pair + 2)
                n = slice(2 * pair * CH, 2 * (pair + 1) * CH)
                S.activation(std[:, n], mv[:, n, 1], ACT.Sqrt, bias=eps_c[:, 0:1]).then_inc(std_ready, 1)

            def normalise(bb):
                act.wait_ge(rstd_ready, bb // 2 + 1)
                for j in range(ACT_J):
                    n = bb * CH + j
                    last = S.activation(xn[:, n, 0:D], x_sb[:, bb, j, :], ACT.Identity,
                                        bias=nmr[:, n:n + 1], scale=rstd[:, n:n + 1])
                last.then_inc(xn_ready, 1)

            def upper_x(bb):
                act.wait_ge(xT_done, bb + 1)
                S.copy(x_h[:, :, bb * P:(bb + 1) * P],
                       ps_x[bb % XB][:, :].rearrange("p (j c) -> p j c", j=CH)).then_inc(xH_ready, 1)

            act.wait_ge(eps_ready, 1)
            deviation(0)
            for bb in range(NB):
                normalise(bb)
                if bb % 2 and bb + 1 < NB:
                    deviation(bb // 2 + 1)
                if bb:
                    upper_x(bb - 1)
            upper_x(NB - 1)
            act.wait_ge(vT_done, 1)
            S.copy(v_h[:, 0, :, :], wi[:, 0:2, :])
            S.copy(v_h[:, 1:3, :, :], ps_vT[0][:, :])
            S.copy(v_h[:, 3, :, :], ps_vT[1][:, 0:2 * D]).then_inc(vH_ready, 1)
            act.wait_ge(lam_ready, 1)
            S.mul(decay[:], pw[:, 1, 1, 0:1].broadcast_to([P, COLS]), mag[:, 1:2]).then_inc(decay_ready, 1)
            act.wait_ge(row_in, 16 * 3)
            S.mul(g_row[:], g_row[:], 0.5).then_inc(row_ready, 1)
            S.mul(b_row[:], b_row[:], 0.5).then_inc(row_ready, 1)
            act.wait_ge(wmid_in, 16)
            for l in range(1, CH + 1):
                S.mul(wtmp[:, 0, l - 1, :], wm[:, 1, :], glam[:, 2, l:l + 1])
                last = S.mul(wtmp[:, 1, l - 1, :], wm[:, 1, :], glam[:, 1, l:l + 1])
            last.then_inc(wtmp_ready, 1)
            for c in range(NWCH):
                cols = slice(c * WCH, (c + 1) * WCH)
                act.wait_ge(up_in[c * UP_DMA // NWCH], 16)
                S.copy(up_h[:, cols], up_l[:, cols].bitcast(F32)).then_inc(wH_ready, 1)
            act.wait_ge(m0_ready, 1)
            S.copy(m_h[:, 0, :], m_0)
            S.copy(m_h[:, 1:CH, :], ps_m[:, D:CH * D]).then_inc(mH_ready, 1)

            def block_step(b, first, last):
                if b <= last:
                    act.wait_ge(o_done, b + 1)
                    if b >= 4:
                        act.wait_ge(y_ready, b - 3)
                    if b == 1:
                        act.wait_ge(tex_ready, 1)
                    S.activation(outT[:, b % 4, :], ps_o[b % 2][:, :], ACT.Identity,
                                 bias=obias[:, b % CH:b % CH + 1]).then_inc(outT_ready, 1)
                k = b - 1
                if first <= k <= last:
                    act.wait_ge(w1_done, k + 1)
                    if k >= 2:
                        act.wait_ge(w2_done, k - 1)
                    S.activation(g1[:, k % 2, :], ps_1[k % 2][:, :], ACT.Gelu,
                                 bias=w1b_c[:, 0:1]).then_inc(g1_ready, 1)
                k = b - 3
                if first <= k <= last:
                    act.wait_ge(yT_done, k + 1)
                    S.copy(s_blk(k), q3(ps_y[k % 2][:, :])).then_inc(ytok_ready, 1)

            for b in range(CH + 1):
                block_step(b, 0, CH - 1)

            def step(t, s):
                if s + 1 < NTILE:
                    act.wait_ge(xsT_done, t + 2)
                    S.copy(xs_h[:, (s + 1) % 2, :], ps_xs[(s + 1) % 2][:, 0:P]).then_inc(xsH_ready, 1)
                if s < NTILE:
                    act.wait_ge(up_done, t + 1)
                    if s >= 2:
                        act.wait_ge(hT_done, t - 1)
                    S.activation(hid[:, s % 2, :], ps_up[s % 2][:, :], ACT.Gelu_apprx_tanh).then_inc(hid_ready, 1)
                if 0 <= s - 1 < NTILE:
                    act.wait_ge(hT_done, t)
                    if s >= 3:
                        act.wait_ge(down_done, t - 2)
                    S.copy(ht[:, (s - 1) % 2, :], ps_hT[(s - 1) % 2][:, :]).then_inc(ht_ready, 1)
                if s == NTILE + 1:
                    block_step(CH, CH, NBLK - 1)
                if s >= 2:
                    act.wait_ge(down_done, t - 1)
                    S.activation(th[:, s % 2, :], ps_dn[s % 2][:, 0:D], ACT.Tanh, scale=0.5).then_inc(th_ready, 1)

            act.wait_ge(xsT_done, 1)
            S.copy(xs_h[:, 0, :], ps_xs[0][:, 0:P]).then_inc(xsH_ready, 1)
            block_step(CH + 1, 0, CH - 1)
            for t in range(HEAD):
                step(t, t)
                if t == 0:
                    block_step(CH + 2, 0, CH - 1)
            with act.Fori(0, ROUNDS) as i:
                for u in range(RING):
                    step(i * RING + HEAD + u, HEAD + u)
            for t in range(HEAD + ROUNDS * RING, NTILE + 2):
                step(t, t)

            def normalise_s(k):
                act.wait_ge(frstd_ready, k + 1)
                for q in range(HALF):
                    n = k * HALF + q
                    last = S.activation(s_blk(k)[:, q, :], s_blk(k)[:, q, :], ACT.Identity,
                                        bias=fnmr[:, n:n + 1], scale=frstd[:, n:n + 1])
                last.then_inc(sn_ready, 1)

            for b in range(CH + 1, NBLK + 3):
                block_step(b, CH, NBLK - 1)
                if CH <= b - 4 < NBLK - 1:
                    normalise_s(b - 4)

        @block.vector
        def _(dve):
            V = nc.vector
            count = [0]

            def mark(ins):
                count[0] += 1
                ins.then_inc(dve_step, 1)

            def settle():
                dve.wait_ge(dve_step, count[0])

            def link(ins):
                mark(ins)
                settle()

            def lower(dst, whole, upper):
                return V.tensor_tensor(dst, whole, upper.bitcast(F32), ALU.subtract)

            def stats(bb):
                dve.wait_ge(x_in[bb], 16)
                for j in range(CH):
                    mark(V.bn_stats(st[:, bb * CH + j, :], x_sb[:, bb, j, :]))
                settle()
                for j in range(CH):
                    last = V.bn_aggr(mv[:, bb * CH + j, :], st[:, bb * CH + j, :])
                last.then_inc(stat_ready, 1)

            def lower_x(bb):
                dve.wait_ge(xH_ready, bb + 1)
                lower(x_l[:, :, bb * P:(bb + 1) * P], ps_x[bb % XB][:, :].rearrange("p (j c) -> p j c", j=CH),
                      x_h[:, :, bb * P:(bb + 1) * P]).then_inc(xL_ready, 1)

            def inverse_std(pair):
                dve.wait_ge(std_ready, pair + 1)
                n = slice(2 * pair * CH, 2 * (pair + 1) * CH)
                link(V.reciprocal(rstd[:, n], std[:, n]))
                V.scalar_tensor_tensor(out=nmr[:, n], in0=mv[:, n, 0], scalar=-1.0, in1=rstd[:, n],
                                       op0=ALU.mult, op1=ALU.mult).then_inc(rstd_ready, 1)

            stats(0)
            stats(1)
            dve.wait_ge(exp_ready, 1)
            link(V.tensor_scalar(angi[:], pexp[:, 1:2], 1.0 / TWO_PI, None, ALU.mult))
            link(V.tensor_copy(ang[:, 0:1], angi[:]))
            link(V.scalar_tensor_tensor(out=ang[:, 1:2], in0=ang[:, 0:1], scalar=-TWO_PI_HI, in1=pexp[:, 1:2],
                                        op0=ALU.mult, op1=ALU.add))
            link(V.scalar_tensor_tensor(out=ang[:, 2:3], in0=ang[:, 0:1], scalar=-TWO_PI_LO, in1=ang[:, 1:2],
                                        op0=ALU.mult, op1=ALU.add))
            link(V.tensor_scalar(ang[:, 5:6], ang[:, 2:3], 3.1415925, -3.1415925, ALU.min, ALU.max))
            link(V.scalar_tensor_tensor(out=ang[:, 3:4], in0=ang[:, 5:6], scalar=-1.0, in1=ang[:, 5:6],
                                        op0=ALU.mult, op1=ALU.max))
            V.tensor_scalar(ang[:, 4:5], ang[:, 3:4], -1.0, TWO_PI / 4, ALU.mult, ALU.add).then_inc(ang_ready, 1)
            stats(2)
            inverse_std(0)
            stats(3)
            dve.wait_ge(wgH_ready, 1)
            lower(wg_l, wg[:], wg_h).then_inc(wgL_ready, 1)
            stats(4)
            inverse_std(1)
            stats(5)
            lower_x(0)
            stats(6)
            lower_x(1)
            inverse_std(2)
            stats(7)
            lower_x(2)
            inverse_std(3)
            lower_x(3)
            dve.wait_ge(tvp_ready, 1)
            for l in range(1, CH):
                V.scalar_tensor_tensor(out=tv[:, l - 1, 0, :], in0=wT[:, 0, :], scalar=pw[:, 1, 1, l:l + 1],
                                       in1=tvp[:, l - 1, 0, :], op0=ALU.mult, op1=ALU.subtract)
                last = V.scalar_tensor_tensor(out=tv[:, l - 1, 1, :], in0=wT[:, 0, :], scalar=pw[:, 2, 1, l:l + 1],
                                              in1=tvp[:, l - 1, 1, :], op0=ALU.mult, op1=ALU.add)
            last.then_inc(tv_ready, 1)
            for bb in range(4, NB):
                lower_x(bb)

            dve.wait_ge(vH_ready, 1)
            lower(v_l[:, 0, :, :], wi[:, 0:2, :], v_h[:, 0, :, :])
            lower(v_l[:, 1:3, :, :], ps_vT[0][:, :], v_h[:, 1:3, :, :])
            lower(v_l[:, 3, :, :], ps_vT[1][:, 0:2 * D], v_h[:, 3, :, :]).then_inc(vL_ready, 1)

            dve.wait_ge(logits_done, 1)
            dve.wait_ge(row_in, 16 * 3)
            dve.wait_ge(const_ready, 1)
            parts = ps_lg[:, :].rearrange("p (n a e) -> p n a e", a=2, e=E)
            link(V.tensor_tensor(lg, parts[:, :, 0, :], bg_row[:].unsqueeze(1).broadcast_to([P, NT, E]), ALU.add))
            link(V.tensor_tensor(lg, lg, parts[:, :, 1, :], ALU.add))
            link(V.tensor_reduce(top[:], lg, AX_X, ALU.max))
            link(V.tensor_tensor(cand, lg, top[:].unsqueeze(2).broadcast_to([P, NT, E]), ALU.is_equal))
            link(V.tensor_tensor(cand, cand, e_minus[:].unsqueeze(1).broadcast_to([P, NT, E]), ALU.mult))
            link(V.tensor_reduce(pick[:], cand, AX_X, ALU.min))
            V.tensor_tensor(onehot, pick[:].unsqueeze(1).broadcast_to([P, E, NT]),
                            e_minus[:].unsqueeze(2).broadcast_to([P, E, NT]), ALU.is_equal).then_inc(onehot_ready, 1)
            dve.wait_ge(count_done, 1)
            before = ps_rt[:, 0:E * NT].rearrange("p (e n) -> p e n", e=E)
            link(V.tensor_copy(aug[:, :, 1:NT + 1], ps_rt[:, E * NT:2 * E * NT].rearrange("p (e n) -> p e n", e=E)))
            link(V.tensor_reduce(cnt[:], aug[:, :, 1:NT + 1], AX_X, ALU.add))
            link(V.tensor_scalar(cnti[:], cnt[:], float(P - 1), None, ALU.add))
            link(V.tensor_scalar(cnti[:], cnti[:], 7, 7, ALU.logical_shift_right, ALU.logical_shift_left))
            mark(V.memset(aug[:, 0, 0:1], 0.0))
            link(V.tensor_tensor(aug[:, 1:E, 0], cnti[:, 0:E - 1], cnt[:, 0:E - 1], ALU.subtract))
            link(V.tensor_tensor_scan(base.rearrange("p e n -> p (e n)"), ones_f,
                                      aug.rearrange("p e n -> p (e n)"), 0.0, ALU.mult, ALU.add))
            link(V.tensor_tensor(posm, before, base[:, :, 0:NT], ALU.add))
            link(V.tensor_tensor(posm, posm, onehot, ALU.mult))
            link(V.tensor_reduce(slot_f[:], posm.rearrange("p e n -> p n e"), AX_X, ALU.add))
            V.tensor_copy(slot[:], slot_f[:]).then_inc(slot_ready, 1)
            def rotate(hf):
                vr, vi = ps_v[hf]
                br, bi = vbias[:, 0:1], vbias[:, 1:2]
                dve.wait_ge(vin_done, 2 * hf + 2)
                if hf:
                    dve.wait_ge(carry_ready, 2 * hf)
                for dst, src, b, tb in ((ra, vr, br, cosk), (rb, vi, bi, sink), (rc, vi, bi, cosk), (rd, vr, br, sink)):
                    last = V.scalar_tensor_tensor(out=bk(dst), in0=bk(src[:]), scalar=b, in1=over_b(tb),
                                                  op0=ALU.add, op1=ALU.mult)
                last.then_inc(rot_ready, 1)

            def scan(hf):
                dve.wait_ge(rot_ready, hf + 1)
                mark(V.tensor_tensor(ra, ra, rb, ALU.add))
                link(V.tensor_tensor(rc, rc, rd, ALU.subtract))
                mark(V.tensor_tensor_scan(rb, decay[:], ra, 0.0, ALU.mult, ALU.add))
                mark(V.tensor_tensor_scan(rd, decay[:], rc, 0.0, ALU.mult, ALU.add))

            def rotate_back_products(hf, c):
                tab_r, tab_i = ((cosk, sink), (sink, cosk))[c]
                settle()
                if c:
                    dve.wait_ge(carry_ready, 2 * hf + 1)
                mark(V.tensor_tensor(bk(ra), bk(rb), over_b(tab_r), ALU.mult))
                mark(V.tensor_tensor(bk(rc), bk(rd), over_b(tab_i), ALU.mult))

            def rotate_back_sum(hf, c):
                settle()
                V.tensor_tensor(bk(carry[:, c, hf * COLS:(hf + 1) * COLS])[:, :, 1:K], bk(ra)[:, :, 0:K - 1],
                                bk(rc)[:, :, 0:K - 1], (ALU.subtract, ALU.add)[c]).then_inc(carry_ready, 1)

            def rotate_back(hf, c):
                rotate_back_products(hf, c)
                rotate_back_sum(hf, c)

            dve.wait_ge(table_ready, 1)
            rotate(0)
            def carry_weights(l):
                dve.wait_ge(wtmp_ready, 1)
                V.scalar_tensor_tensor(out=b_w[:, l - 1, :], in0=wm[:, 0, :], scalar=glam[:, 1, l:l + 1],
                                       in1=wtmp[:, 0, l - 1, :], op0=ALU.mult, op1=ALU.subtract)
                V.scalar_tensor_tensor(out=c_w[:, l - 1, :], in0=wm[:, 0, :], scalar=glam[:, 0, l:l + 1],
                                       in1=wtmp[:, 1, l - 1, :], op0=ALU.mult, op1=ALU.subtract).then_inc(bc_ready, 1)

            scan(0)
            dve.wait_ge(m_done, 1)
            V.tensor_tensor(m_0, ps_m[:, 0:D], wi[:, 2, :], ALU.add).then_inc(m0_ready, 1)
            rotate_back(0, 0)
            dve.wait_ge(mH_ready, 1)
            dve.wait_ge(m0_ready, 1)
            lower(m_l[:, 0, :], m_0, m_h[:, 0, :])
            lower(m_l[:, 1:CH, :], ps_m[:, D:CH * D], m_h[:, 1:CH, :])
            V.tensor_tensor_scan(obias[:], pw[:, 1, 1, 0:1].broadcast_to([P, CH]), ps_mb[:, 0:CH], bm[:, 0:1],
                                 ALU.mult, ALU.add).then_inc(mL_ready, 1)
            rotate_back(0, 1)
            for l in range(1, CH + 1):
                carry_weights(l)
            rotate(1)

            def lower_w(c):
                cols = slice(c * WCH, (c + 1) * WCH)
                dve.wait_ge(wH_ready, c + 1)
                lower(up_l[:, cols], up_l[:, cols].bitcast(F32), up_h[:, cols]).then_inc(wL_ready, 1)

            def block_step(b, first, last):
                k = b - 2
                if first <= k <= last:
                    dve.wait_ge(w2_done, k + 1)
                    if k >= 2:
                        dve.wait_ge(yT_done, k - 1)
                    V.scalar_tensor_tensor(out=yT[:, k % 2, :], in0=ps_2[k % 2][:, :], scalar=w2b_c[:, 0:1],
                                           in1=outT[:, k % 4, :], op0=ALU.add, op1=ALU.add).then_inc(y_ready, 1)
                k = b - 3
                if first <= k <= last:
                    dve.wait_ge(ytok_ready, k + 1)
                    for q in range(HALF):
                        mark(V.bn_stats(fst[:, k * HALF + q, :], s_blk(k)[:, q, :]))
                    settle()
                    for q in range(HALF):
                        fin = V.bn_aggr(fmv[:, k * HALF + q, :], fst[:, k * HALF + q, :])
                    fin.then_inc(fstat_ready, 1)

            link(V.tensor_tensor(tcmp, tile_at[:].unsqueeze(2).broadcast_to([P, NTILE, E - 1]),
                                 base[:, 1:E, 0].unsqueeze(1).broadcast_to([P, NTILE, E - 1]), ALU.is_ge))
            dve.wait_ge(const_ready, 1)
            link(V.tensor_reduce(tex_f[:].rearrange("p m i -> p (m i)")[:, 0:NTILE], tcmp, AX_X, ALU.add))
            link(V.tensor_tensor(tex_f[:], tex_f[:], eights[:].unsqueeze(1).broadcast_to([P, NWORD + 1, RING]),
                                 ALU.mult))
            link(V.tensor_reduce(tex_r[:], tex_f[:], AX_X, ALU.add))
            V.scalar_tensor_tensor(out=tex[:], in0=tex_r[:, 1:NWORD + 1, 0], scalar=float(E ** RING),
                                   in1=tex_r[:, 0:NWORD, 0], op0=ALU.mult, op1=ALU.add).then_inc(tex_ready, 1)
            for c in range(NWCH):
                lower_w(c)
            for b in range(2, CH + 1):
                block_step(b, 0, CH - 1)

            def lower_xs(t, s):
                dve.wait_ge(xsH_ready, t + 1)
                V.tensor_copy(token[:, bass.ds(t, 1)], xs_in[:, s % RING, D:D + 1].bitcast(I32))
                lower(xs_l[:, s % 2, :], ps_xs[s % 2][:, 0:P], xs_h[:, s % 2, :]).then_inc(xsL_ready, 1)

            def silu2(t, s, rnd):
                dve.wait_ge(th_ready, t + 1)
                if s >= RING:
                    dve.wait_ge(gate_out[s % RING], rnd * 16)
                V.scalar_tensor_tensor(out=gate[:, s % RING, :], in0=th[:, s % 2, :], scalar=1.0,
                                       in1=ps_dn[s % 2][:, 0:D], op0=ALU.add, op1=ALU.mult).then_inc(gate_ready, 1)

            def step(t, s, rnd):
                if s + 1 < NTILE:
                    lower_xs(t + 1, s + 1)
                if s >= 2:
                    silu2(t - 2, s - 2, rnd)

            lower_xs(0, 0)
            block_step(CH + 1, 0, CH - 1)
            for t in range(HEAD):
                step(t, t, (t - 2) // RING)
                if t == 0:
                    block_step(CH + 2, 0, CH - 1)
                elif t == 2:
                    dve.wait_ge(rot_ready, 2)
                    mark(V.tensor_tensor(ra, ra, rb, ALU.add))
                    mark(V.tensor_tensor(rc, rc, rd, ALU.subtract))
                elif t == 3:
                    settle()
                    mark(V.tensor_tensor_scan(rb, decay[:], ra, 0.0, ALU.mult, ALU.add))
                    mark(V.tensor_tensor_scan(rd, decay[:], rc, 0.0, ALU.mult, ALU.add))
                elif t in (4, 7):
                    rotate_back_products(1, (t - 4) // 3)
                elif t in (5, 8):
                    rotate_back_sum(1, (t - 5) // 3)
            with dve.Fori(0, ROUNDS) as i:
                for u in range(RING):
                    step(i * RING + HEAD + u, HEAD + u, i + (HEAD + u - 2) // RING)
            for t in range(HEAD + ROUNDS * RING, NTILE + 2):
                step(t, t, (t - 2) // RING)

            def prepare(k):
                j = k - CH
                gk, xk, t = gate_in[:, HALF:NB, j, :], x_sb[:, HALF:NB, j, :], q3(rot[:, j, :])
                mark(V.tensor_tensor(t, gk, b_row[:].unsqueeze(1).broadcast_to([P, HALF, D]), ALU.mult))
                settle()
                mark(V.tensor_tensor(xk, xk, t, ALU.add))
                mark(V.tensor_tensor(gk, gk, g_row[:].unsqueeze(1).broadcast_to([P, HALF, D]), ALU.mult))

            def finish(k):
                j = k - CH
                y, xk = s_blk(k), x_sb[:, HALF:NB, j, :]
                settle()
                if k < NBLK - 1:
                    dve.wait_ge(sn_ready, j + 1)
                    link(V.tensor_tensor(y, y, gate_in[:, HALF:NB, j, :], ALU.mult))
                    V.tensor_tensor(xk, xk, y, ALU.add).then_inc(half1_ready, 1)
                    return
                for q in range(HALF):
                    mark(V.scalar_tensor_tensor(out=y[:, q, :], in0=y[:, q, :], scalar=fmv[:, k * HALF + q, 0:1],
                                                in1=gate_in[:, HALF + q, j, :], op0=ALU.subtract, op1=ALU.mult))
                dve.wait_ge(frstd_ready, k + 1)
                settle()
                for q in range(HALF):
                    last = V.scalar_tensor_tensor(out=xk[:, q, :], in0=y[:, q, :],
                                                  scalar=frstd[:, k * HALF + q:k * HALF + q + 1],
                                                  in1=xk[:, q, :], op0=ALU.mult, op1=ALU.add)
                last.then_inc(half1_ready, 1)

            dve.wait_ge(row_ready, 2)
            for bb in range(HALF, NB):
                dve.wait_ge(gate_ld[bb], 16)
            prepare(CH)
            prepare(CH + 1)
            block_step(CH + 2, CH, NBLK - 1)
            prepare(CH + 2)
            prepare(CH + 3)
            for b in range(CH + 3, NBLK + 3):
                block_step(b, CH, NBLK - 1)
                if b - 4 >= CH:
                    finish(b - 4)
            finish(NBLK - 1)

        @block.tensor
        def _(pe):
            mm, tr = nc.tensor.matmul, nc.tensor.transpose

            def mm3(dst, a_h, a_l, b_h, b_l, start, stop):
                mm(dst, a_h, b_h, start=start, stop=False)
                mm(dst, a_h, b_l, start=False, stop=False)
                return mm(dst, a_l, b_h, start=False, stop=stop)

            pe.wait_ge(const_ready, 1)
            pe.wait_ge(win_in, 16 * 2)
            tr(ps_wT[:, 0:D], wi[:, 0, :], ident[:])
            tr(ps_wT[:, D:2 * D], wi[:, 1, :], ident[:]).then_inc(wT_done, 1)

            def logits(bb):
                pe.wait_ge(xL_ready, bb + 1)
                for j in range(CH):
                    n = bb * CH + j
                    tok = slice(bb * P, (bb + 1) * P)
                    dst = ps_lg[:, 2 * n * E:2 * (n + 1) * E]
                    mm(dst, x_h[:, j, tok], wg_hl[:, :], start=True, stop=False)
                    last = mm(dst[:, 0:E], x_l[:, j, tok], wg_h, start=False, stop=True)
                return last

            def busy(n):
                for _ in range(n):
                    mm(ps_rt[:, 0:P], ones_b[:], ones_b[:], start=True, stop=True)

            pe.wait_ge(wgL_ready, 1)
            for bb in range(NB):
                busy(WARM)
                pe.wait_ge(xn_ready, bb + 1)
                pe.wait_ge(xnp_ready, bb + 1)
                if bb >= XB:
                    pe.wait_ge(xL_ready, bb - XB + 1)
                for j in range(CH):
                    last = tr(ps_x[bb % XB][:, j * P:(j + 1) * P], xn[:, bb * CH + j, 0:D], ident[:])
                last.then_inc(xT_done, 1)
                if bb >= 3:
                    logits(bb - 3)
            pe.wait_ge(tv_ready, 1)
            for i in range(2 * (CH - 1)):
                l, c = divmod(i, 2)
                last = tr(ps_vT[i // 4][:, (i % 4) * D:(i % 4 + 1) * D], tv[:, l, c, :], ident[:])
            last.then_inc(vT_done, 1)
            logits(NB - 3)
            logits(NB - 2)
            logits(NB - 1).then_inc(logits_done, 1)

            pe.wait_ge(vL_ready, 1)
            def chunk_sums(hf, c):
                cols = slice(hf * COLS, (hf + 1) * COLS)
                for i in range(CH):
                    l = CH - 1 - i
                    last = mm3(ps_v[hf][c][:, :], v_h[:, l, c, :], v_l[:, l, c, :], x_h[:, i, cols], x_l[:, i, cols],
                               start=(i == 0), stop=(i == CH - 1))
                last.then_inc(vin_done, 1)

            chunk_sums(0, 0)
            pe.wait_ge(onehot_ready, 1)
            hot = onehot.rearrange("p e n -> p (e n)")
            mm(ps_rt[:, 0:E * NT], tri[:], hot, start=True, stop=True)
            mm(ps_rt[:, E * NT:2 * E * NT], ones_b[:], hot, start=True, stop=True).then_inc(count_done, 1)
            chunk_sums(0, 1)
            pe.wait_ge(gw_ready, 1)
            for l in range(CH):
                w = wT[:, :, :] if l == 0 else tv[:, l - 1, :, :]
                mm(ps_m[:, l * D:(l + 1) * D], w[:, 0, :], gw[:, 0, :], start=True, stop=False)
                mm(ps_m[:, l * D:(l + 1) * D], w[:, 1, :], gw[:, 1, :], start=False, stop=True)
            mm(ps_mb[:, 0:CH], gw[:, 0, :], lamb[:, 0, :], start=True, stop=False)
            mm(ps_mb[:, 0:CH], gw[:, 1, :], lamb[:, 1, :], start=False, stop=True).then_inc(m_done, 1)
            chunk_sums(1, 0)
            chunk_sums(1, 1)
            pe.wait_ge(mL_ready, 1)

            def block_step(b, first, last):
                if b <= last:
                    hf, j = divmod(b, CH)
                    cols = slice(hf * COLS, (hf + 1) * COLS)
                    o = ps_o[b % 2][:, :]
                    if b >= 2:
                        pe.wait_ge(outT_ready, b - 1)
                    if b == CH:
                        pe.wait_ge(xsL_ready, NTILE)
                    for i in range(j + 1):
                        mm3(o, m_h[:, j - i, :], m_l[:, j - i, :], x_h[:, i, cols], x_l[:, i, cols],
                            start=(i == 0), stop=False)
                    pe.wait_ge(carry_ready, 2 * hf + 2)
                    pe.wait_ge(bc_ready, j + 1)
                    mm(o, b_w[:, j, :], carry[:, 0, cols], start=False, stop=False)
                    mm(o, c_w[:, j, :], carry[:, 1, cols], start=False, stop=True).then_inc(o_done, 1)
                k = b - 1
                if first <= k <= last:
                    pe.wait_ge(outT_ready, k + 1)
                    mm(ps_1[k % 2][:, :], w1s, outT[:, k % 4, :], start=True, stop=True).then_inc(w1_done, 1)
                k = b - 2
                if first <= k <= last:
                    pe.wait_ge(g1_ready, k + 1)
                    if k == 0:
                        pe.wait_ge(rot_ready, 2)
                    if k >= 2:
                        pe.wait_ge(y_ready, k - 1)
                    mm(ps_2[k % 2][:, :], w2s, g1[:, k % 2, :], start=True, stop=True).then_inc(w2_done, 1)
                k = b - 3
                if first <= k <= last:
                    pe.wait_ge(y_ready, k + 1)
                    if k >= 2:
                        pe.wait_ge(ytok_ready, k - 1)
                    for q in range(HALF):
                        fin = tr(ps_y[k % 2][:, q * P:(q + 1) * P], yT[:, k % 2, q * P:(q + 1) * P], ident[:])
                    fin.then_inc(yT_done, 1)

            for b in range(CH + 1):
                block_step(b, 0, CH - 1)


            def transpose_x(t, s, rnd):
                r = s % RING
                pe.wait_ge(xs_ld[r], rnd * 16 + 16)
                tr(ps_xs[s % 2][:, 0:P], xs_in[:, r, 0:D], ident[:]).then_inc(xsT_done, 1)

            def experts(m):
                word = pe.value_load(tex[0:1, bass.ds(m, 1)], min_val=0, max_val=E ** 8 - 1)
                return [((word >> (3 * i)) & (E - 1)) * H for i in range(8)]

            def up(t, s, e):
                dst, a_h, a_l = ps_up[s % 2][:, :], xs_h[:, s % 2, :], xs_l[:, s % 2, :]
                pe.wait_ge(xsL_ready, t + 1)
                mm3(dst, a_h, a_l, up_h[:, bass.ds(e, H)], up_l[:, bass.ds(e, H)],
                    start=True, stop=True).then_inc(up_done, 1)

            def transpose_h(t, s):
                pe.wait_ge(hid_ready, t + 1)
                for c in range(HC):
                    last = tr(ps_hT[s % 2][:, c * P:(c + 1) * P], hid[:, s % 2, c * P:(c + 1) * P], ident[:])
                last.then_inc(hT_done, 1)

            def down(t, s, e):
                dst = ps_dn[s % 2][:, 0:D]
                pe.wait_ge(ht_ready, t + 1)
                if s >= 2:
                    pe.wait_ge(gate_ready, t - 1)
                for c in range(HC):
                    last = mm(dst, ht[:, s % 2, c * P:(c + 1) * P], down_w[:, bass.ds(e + c * D, D)],
                              start=(c == 0), stop=(c == HC - 1))
                last.then_inc(down_done, 1)

            def first_part(t, s, rnd, e):
                if s + 1 < NTILE:
                    transpose_x(t + 1, s + 1, rnd)
                if s < NTILE:
                    up(t, s, e)
                if 0 <= s - 1 < NTILE:
                    transpose_h(t - 1, s - 1)

            def steps(t0, s0, n, m, rnd_of, between=None):
                e = experts(m)
                lo = RING * ((s0 - 2) // RING) if s0 else 0
                for u in range(n):
                    s = s0 + u
                    if between:
                        between(s)
                    if s >= 2:
                        down(t0 + u - 2, s - 2, e[s - 2 - lo])
                    first_part(t0 + u + 1, s + 1, rnd_of(u), e[s + 1 - lo] if s + 1 < NTILE else None)

            def head(s):
                if s == 0:
                    block_step(CH + 2, 0, CH - 1)
                elif s == 2:
                    pe.wait_ge(down_in, 16)
                    pe.wait_ge(ytok_ready, CH)

            def tail(s):
                if s == NTILE + 1:
                    block_step(CH, CH, NBLK - 1)

            pe.wait_ge(outT_ready, CH)
            transpose_x(0, 0, 0)
            block_step(CH + 1, 0, CH - 1)
            pe.wait_ge(tex_ready, 1)
            pe.wait_ge(wL_ready, NWCH)
            pe.wait_ge(g1_ready, CH)
            first_part(0, 0, 0, experts(0)[0])
            steps(0, 0, 6, 0, lambda u: (u + 2) // RING, head)
            steps(6, 6, RING, 1, lambda u: (u + 8) // RING)
            with pe.Fori(0, ROUNDS) as i:
                steps(i * RING + HEAD, HEAD, RING, i + (HEAD - 2) // RING, lambda u: i + (HEAD + u + 2) // RING)
            t = HEAD + ROUNDS * RING
            steps(t, t, NTILE + 2 - t, (t - 2) // RING, lambda u: (t + u + 2) // RING, tail)

            pe.wait_ge(hid_ready, NTILE)
            pe.wait_ge(gate_ready, NTILE)
            for b in range(CH + 1, NBLK + 3):
                block_step(b, CH, NBLK - 1)


def kernel(L0_attn_x, L0_attn_W_in, L0_attn_b_in, L0_attn_params_log, L0_attn_W_mid, L0_attn_b_mid,
           L0_attn_w1_w, L0_attn_w1_b, L0_attn_w2_w, L0_attn_w2_b, L0_attn_ln_g, L0_attn_ln_b,
           L0_ffn_W1, L0_ffn_W2, L0_ffn_Wg, L0_ffn_bg):
    import numpy as np
    import concourse.bacc as bacc
    from concourse.bass_utils import run_bass_kernel_spmd

    E, H, D = L0_ffn_W2.shape
    laid_out = {
        "x": L0_attn_x,
        "w_small": np.concatenate([L0_attn_W_in, L0_attn_W_mid, L0_attn_w1_w[None], L0_attn_w2_w[None]]
                                  ).transpose(1, 0, 2),
        "columns": np.concatenate([L0_attn_params_log, L0_attn_b_in, L0_attn_b_mid, L0_attn_w1_b[None],
                                   L0_attn_w2_b[None]]).transpose(1, 0),
        "rows": np.stack([L0_attn_ln_g, L0_attn_ln_b]),
        "w1": np.asarray(L0_ffn_W1).transpose(1, 0, 2),
        "w2": np.asarray(L0_ffn_W2).reshape(E, H // P, P, D).transpose(2, 0, 1, 3),
        "wg": L0_ffn_Wg,
        "bg": L0_ffn_bg,
    }
    nc = bacc.Bacc("TRN2", target_bir_lowering=False, num_devices=1)
    arrays, args = {}, []
    for name, value in laid_out.items():
        a = np.ascontiguousarray(value)
        arrays[f"{name}_dram"] = a
        args.append(nc.dram_tensor(f"{name}_dram", a.shape, mybir.dt.from_np(a.dtype), kind="ExternalInput").ap())
    out = nc.dram_tensor("out_dram", L0_attn_x.shape, F32, kind="ExternalOutput").ap()
    lru_moe(nc, *args, out)
    r = run_bass_kernel_spmd(nc, [arrays], core_ids=[0])
    return r.results[0]["out_dram"]
```

```python
from contextlib import ExitStack

import concourse.bass as bass
from concourse import mybir

P = 128
F32 = mybir.dt.float32
F32R = mybir.dt.float32r
BF16 = mybir.dt.bfloat16
I32 = mybir.dt.int32
ALU = mybir.AluOpType
ACT = mybir.ActivationFunctionType
AX_X = mybir.AxisListType.X

CH = 4
EPS = 1e-5
TWO_PI = 6.283185307179586
TWO_PI_HI = 6.28125
TWO_PI_LO = TWO_PI - TWO_PI_HI


def lru_moe(nc, x, W_small, columns, rows, W1, W2, Wg, bg, out):
    B, T, D = x.shape
    _, E, H = W1.shape
    NB = B * T // (P * CH)
    NT = NB * CH
    K = T // CH
    HALF = NB // 2
    BPH = B // 2
    COLS = BPH * K
    HC = H // P
    NTILE = NT + E - 1
    NTOK = B * T
    RW = D + 4
    RING = 4
    NBLK = 2 * CH
    EARLY = NBLK - 2
    HEAD = 10
    ROUNDS = (NTILE - 2 - HEAD) // RING
    NWORD = -(-NTILE // RING)
    ACT_J = CH - 1
    FIRST = 2
    WARM = 10
    WARM_FIRST = 16
    WARM_CARRY = 40
    XB = 4
    assert D == P and K * 2 == P and H == 512 and E == 8 and NB == 8 and HEAD % RING == 2

    xs_dram = nc.dram_tensor("sorted_rows", (NTILE * P, RW), F32, kind="Internal").ap()
    gate_dram = nc.dram_tensor("gate_rows", (NTOK + RING * P, D), F32, kind="Internal").ap()

    ctx = ExitStack()
    with ctx:
        def sb(name, shape, dt=F32):
            return ctx.enter_context(nc.sbuf_tensor(name, shape, dt))

        def sem(name):
            return ctx.enter_context(nc.semaphore(name))

        bank = [ctx.enter_context(nc.psum_tensor(f"bank{i}", [P, 512], F32)) for i in range(8)]

        x_sb = sb("x_sb", [P, NB, CH, D])
        xn = sb("xn", [P, NT, RW])
        x_h = sb("x_h", [P, CH, NB * P], F32R)
        x_l = sb("x_l", [P, CH, NB * P], F32R)
        w_small = sb("w_small", [P, 7, D])
        wi, wm, w1s, w2s = w_small[:, 0:3, :], w_small[:, 3:5, :], w_small[:, 5, :], w_small[:, 6, :]
        wg = sb("wg", [P, E])
        wg_hl = sb("wg_hl", [P, 2 * E], F32R)
        wg_h, wg_l = wg_hl[:, 0:E], wg_hl[:, E:2 * E]
        up_w = sb("up_w", [P, E * H])
        down_w = sb("down_w", [P, E * H])
        cols_sb = sb("cols_sb", [P, 10])
        plog, bin_c, bmid_c = cols_sb[:, 0:3], cols_sb[:, 3:6], cols_sb[:, 6:8]
        w1b_c, w2b_c = cols_sb[:, 8:9], cols_sb[:, 9:10]
        g_row = sb("g_row", [P, D])
        b_row = sb("b_row", [P, D])
        bg_row = sb("bg_row", [P, E])
        ident = sb("ident", [P, P])
        tri = sb("tri", [P, P], BF16)
        ones_b = sb("ones_b", [P, P], BF16)
        neg_half = sb("neg_half", [P, HALF])
        eps_c = sb("eps_c", [P, 1])
        unread = sb("unread", [P, 1])
        e_minus = sb("e_minus", [P, E])
        tile_at = sb("tile_at", [P, NTILE])
        pexp = sb("pexp", [P, 3])
        mag = sb("mag", [P, 2])
        ang = sb("ang", [P, 6])
        angi = sb("angi", [P, 1], I32)
        pw = sb("pw", [P, 3, 2, CH + 1])
        glam = sb("glam", [P, 3, CH + 1])
        lamb = sb("lamb", [P, 2, CH])
        lamt = sb("lamt", [P, 2, 2, CH])
        gw = sb("gw", [P, 2, D])
        tab = sb("tab", [P, 3, K + 1])
        cosk, sink = tab[:, 1, 0:K], tab[:, 2, 0:K]
        pwt = sb("pwt", [P, 2, 2, 2 * (CH + 1)])
        vbias = sb("vbias", [P, 2])
        wT = sb("wT", [P, 2, D])
        bc_w = sb("bc_w", [P, 2, CH, D])
        b_w, c_w = bc_w[:, 0, :, :], bc_w[:, 1, :, :]
        bc_h = sb("bc_h", [P, 2, CH, D], F32R)
        bc_l = sb("bc_l", [P, 2, CH, D], F32R)
        m_h = sb("m_h", [P, CH, D], F32R)
        m_l = sb("m_l", [P, CH, D], F32R)
        bm = sb("bm", [P, 1])
        obias = sb("obias", [P, CH])
        st = sb("st", [P, NT, 6])
        mv = sb("mv", [P, NT, 2])
        std = sb("std", [P, NT])
        rstd = sb("rstd", [P, NT])
        nmr = sb("nmr", [P, NT])
        fst = sb("fst", [P, NT, 6])
        fmv = sb("fmv", [P, NT, 2])
        fveps = sb("fveps", [P, NT])
        fnmean = sb("fnmean", [P, NT])
        frstd = sb("frstd", [P, NT])
        fnmr = sb("fnmr", [P, NT])
        top = sb("top", [P, NT])
        pick = sb("pick", [P, NT])
        cnt = sb("cnt", [P, E])
        cnti = sb("cnti", [P, E], I32)
        slot_f = sb("slot_f", [P, NT])
        slot = sb("slot", [P, NT], I32)
        tex_f = sb("tex_f", [P, NWORD + 1, RING])
        tex_r = sb("tex_r", [P, NWORD + 1, 1])
        tex = sb("tex", [P, NWORD], I32)
        eights = sb("eights", [P, RING])
        token = sb("token", [P, NTILE], I32)
        rot = sb("rot", [P, 4, COLS])
        ra, rb, rc, rd = rot[:, 0, :], rot[:, 1, :], rot[:, 2, :], rot[:, 3, :]
        tabt = rot[:, 0, 0:4 * (K // 2 + 1)].rearrange("p (a b k) -> p a b k", a=2, b=2)
        ones_f = rot[:, 3, 0:E * (NT + 1)]
        carry_0 = sb("carry_0", [P, 2, COLS])
        carry_h = sb("carry_h", [P, 2, COLS], F32R)
        carry_l = sb("carry_l", [P, 2, COLS], F32R)
        s_sb = sb("s_sb", [P, NB, CH, D])
        fill = sb("fill", [P, RING, RW])
        v_h = sb("v_h", [P, CH, 2, D], F32R)
        v_l = sb("v_l", [P, CH, 2, D], F32R)
        xs_in = sb("xs_in", [P, RING, RW])
        decay = xs_in[:, :, :].rearrange("p r c -> p (r c)")[:, 0:COLS]
        xsT = sb("xsT", [P, 2, P])
        up_t = sb("up_t", [P, 2, H])
        hT = sb("hT", [P, RING, H])
        assert COLS == H
        carry = [carry_0[:, :, :], hT[:, 0:2, :]]
        th = sb("th", [P, 2, D])
        gate = sb("gate", [P, RING, D])
        blk = sb("blk", [P, 8, COLS])
        outT, g1, yT = blk[:, 0:4, :], blk[:, 4:6, :], blk[:, 6:8, :]
        early = blk[:, :, :].rearrange("p a b -> p (a b)")

        def part(at, *shape):
            n = 1
            for d in shape:
                n *= d
            names = " ".join("abc"[:len(shape)])
            return early[:, at:at + n].rearrange(f"p ({names}) -> p {names}", **dict(zip("abc", shape)))

        tv = part(0, CH - 1, 2, D)
        tvp = part(768, CH - 1, 2, D)
        wtmp = part(1536, 2, CH, D)
        lg = part(2816, NT, E)
        posm = part(2816, E, NT)
        cand = part(3072, NT, E)
        aug = part(3328, E, NT + 1)
        base = part(3592, E, NT + 1)
        onehot = early[:, 3856:3856 + E * NT // 2].bitcast(BF16).rearrange("p (e n) -> p e n", e=E)
        tcmp = fill[:, :, :].rearrange("p u c -> p (u c)")[:, 0:NTILE * (E - 1)].rearrange("p (t e) -> p t e", e=E - 1)
        m_0 = part(0, D)[:, :]

        x_in = [sem(f"x_in{i}") for i in range(NB)]
        par_in = sem("par_in")
        win_in = sem("win_in")
        wmid_in = sem("wmid_in")
        row_in = sem("row_in")
        up_in = sem("up_in")
        down_in = sem("down_in")
        const_ready = sem("const_ready")
        pool_step = sem("pool_step")
        dve_step = sem("dve_step")
        act_step = sem("act_step")
        fill_ready = sem("fill_ready")
        eps_ready = sem("eps_ready")
        filled = sem("filled")
        wgH_ready = sem("wgH_ready")
        wgL_ready = sem("wgL_ready")
        exp_ready = sem("exp_ready")
        ang_ready = sem("ang_ready")
        cs_ready = sem("cs_ready")
        lam_ready = sem("lam_ready")
        table_ready = sem("table_ready")
        decay_ready = sem("decay_ready")
        wT_done = sem("wT_done")
        wT_ready = sem("wT_ready")
        tvp_ready = sem("tvp_ready")
        tv_ready = sem("tv_ready")
        vT_done = sem("vT_done")
        vH_ready = sem("vH_ready")
        vL_ready = sem("vL_ready")
        wtmp_ready = sem("wtmp_ready")
        bc_ready = sem("bc_ready")
        bcH_ready = sem("bcH_ready")
        bcL_ready = sem("bcL_ready")
        gw_ready = sem("gw_ready")
        m_done = sem("m_done")
        m0_ready = sem("m0_ready")
        mH_ready = sem("mH_ready")
        mL_ready = sem("mL_ready")
        stat_ready = sem("stat_ready")
        rstd0_ready = sem("rstd0_ready")
        rstd_ready = sem("rstd_ready")
        xn_ready = sem("xn_ready")
        xnp_ready = sem("xnp_ready")
        std_ready = sem("std_ready")
        xT_done = sem("xT_done")
        xH_ready = sem("xH_ready")
        xL_ready = sem("xL_ready")
        logits_done = sem("logits_done")
        onehot_ready = sem("onehot_ready")
        count_done = sem("count_done")
        slot_ready = sem("slot_ready")
        tex_ready = sem("tex_ready")
        vin_done = sem("vin_done")
        rot_ready = sem("rot_ready")
        carry_ready = sem("carry_ready")
        carryH_ready = sem("carryH_ready")
        carryL_ready = sem("carryL_ready")
        o_done = sem("o_done")
        outT_ready = sem("outT_ready")
        w1_done = sem("w1_done")
        g1_ready = sem("g1_ready")
        w2_done = sem("w2_done")
        y_ready = sem("y_ready")
        yT_done = sem("yT_done")
        ytok_ready = sem("ytok_ready")
        fstat_ready = sem("fstat_ready")
        frstd_ready = sem("frstd_ready")
        row_ready = sem("row_ready")
        sorted_out = sem("sorted_out")
        xs_ld = [sem(f"xs_ld{i}") for i in range(RING)]
        xsT_done = sem("xsT_done")
        xsT_ready = sem("xsT_ready")
        upw_ready = sem("upw_ready")
        up_done = sem("up_done")
        hT_ready = sem("hT_ready")
        down_done = sem("down_done")
        th_ready = sem("th_ready")
        gate_ready = sem("gate_ready")
        gate_out = [sem(f"gate_out{i}") for i in range(RING)]
        gate_ld = [sem(f"gate_ld{i}") for i in range(NB)]
        early_ready = sem("early_ready")
        sn_ready = sem("sn_ready")
        xbias_ready = sem("xbias_ready")
        half0_ready = sem("half0_ready")
        group1_ready = sem("group1_ready")
        half1_ready = sem("half1_ready")
        stored = sem("stored")

        ps_wT = bank[4]
        ps_vT = [bank[4], bank[6]]
        ps_x = [bank[0], bank[1], bank[7], bank[5]]
        ps_lg = bank[2]
        ps_rt = bank[3]
        ps_v = [[bank[4], bank[5]], [bank[6], bank[7]]]
        ps_m, ps_mb = bank[0], bank[1]
        ps_o = [bank[0], bank[1]]
        ps_1 = [bank[2], bank[3]]
        ps_2 = [bank[6], bank[7]]
        ps_y = [bank[4], bank[5]]
        par = EARLY % 2
        ps_xs = [bank[par], bank[2 + par]]
        ps_up = [bank[1 - par], bank[3 - par]]
        ps_dn = [bank[4 + par], bank[5 - par]]

        x_dram = x.rearrange("b t d -> (b t) d").rearrange("(g p j) d -> g p j d", p=P, j=CH)
        out_dram = out.rearrange("b t d -> (b t) d").rearrange("(g p j) d -> g p j d", p=P, j=CH)
        gate_v = gate_dram[0:NTOK, :].rearrange("(g p j) d -> g p j d", p=P, j=CH)
        gate_in = xn[:, :, 0:D].rearrange("p (g j) d -> p g j d", j=CH)
        up_dram, down_dram = W1.rearrange("d e h -> d (e h)"), W2.rearrange("p e c d -> p (e c d)")

        def bk(ap):
            return ap.rearrange("p (b k) -> p b k", k=K)

        def over_b(tab):
            return tab.unsqueeze(1).broadcast_to([P, BPH, K])

        def s_blk(b):
            hf, j = divmod(b, CH)
            return s_sb[:, hf * HALF:(hf + 1) * HALF, j, :]

        def q3(ap):
            return ap.rearrange("p (q d) -> p q d", d=D)

        def experts(eng, m):
            word = eng.value_load(tex[0:1, bass.ds(m, 1)], min_val=0, max_val=E ** 8 - 1)
            return [((word >> (3 * i)) & (E - 1)) * H for i in range(8)]

        block = ctx.enter_context(nc.Block())

        @block.sync
        def _(sp):
            for bb in range(NB):
                sp.dma_start(x_sb[:, bb, :, :], x_dram[bb]).then_inc(x_in[bb], 16)
                if bb == 1:
                    sp.dma_start(wg[:, :], Wg).then_inc(win_in, 16)
            sp.dma_start(w_small[:, 3:7, :], W_small[:, 3:7, :]).then_inc(wmid_in, 16)
            sp.dma_start(bg_row[:, :], bg.rearrange("(a d) -> a d", a=1).broadcast_to([P, E])).then_inc(row_in, 16)
            sp.dma_start(g_row[:, :], rows[0:1, :].broadcast_to([P, D])).then_inc(row_in, 16)
            sp.dma_start(b_row[:, :], rows[1:2, :].broadcast_to([P, D])).then_inc(row_in, 16)
            sp.wait_ge(fill_ready, 1)
            rounds = NTILE // RING
            whole = rounds * RING * P
            for u in range(RING):
                sp.dma_start(xs_dram[0:whole, :].rearrange("(i u p) c -> u p i c", u=RING, p=P)[u],
                             fill[:, u, :].unsqueeze(1).broadcast_to([P, rounds, RW])).then_inc(filled, 16)
            sp.dma_start(xs_dram[whole:NTILE * P, :].rearrange("(u p) c -> p u c", p=P),
                         fill[:, 0:NTILE - rounds * RING, :]).then_inc(filled, 16)
            sp.dma_start(up_w[:, :], up_dram).then_inc(up_in, 16)
            sp.dma_start(down_w[:, :], down_dram).then_inc(down_in, 16)

            sp.wait_ge(sorted_out, 16 * NT)
            sp.wait_ge(carry_ready, 4)

            def load(t, r):
                sp.dma_start(xs_in[:, r, :], xs_dram[bass.ds(t * P, P), :]).then_inc(xs_ld[r], 16)

            for t in range(RING):
                load(t, t)
            rounds = NTILE // RING - 1
            with sp.Fori(0, rounds) as i:
                for u in range(RING):
                    sp.wait_ge(xsT_ready, i * RING + u + 1)
                    load(i * RING + u + RING, u)
            for t in range((rounds + 1) * RING, NTILE):
                sp.wait_ge(xsT_ready, t - RING + 1)
                load(t, t % RING)

            for r in range(RING):
                sp.wait_ge(gate_out[r], 16 * ((NTILE - r + RING - 1) // RING))
            for bb in [0, 1, *range(HALF, NB), *range(2, HALF)]:
                sp.dma_start(gate_in[:, bb, :, :], gate_v[bb]).then_inc(gate_ld[bb], 16)
            for i, bb in enumerate([1, 0, *range(2, HALF)]):
                if bb == 1:
                    sp.wait_ge(group1_ready, 1)
                else:
                    sp.wait_ge(half0_ready, i)
                sp.dma_start(out_dram[bb], x_sb[:, bb, :, :]).then_inc(stored, 16)
            sp.wait_ge(stored, 16 * (HALF + CH))

        @block.gpsimd
        def _(pool):
            G = nc.gpsimd
            count = [0]

            def mark(ins):
                count[0] += 1
                ins.then_inc(pool_step, 1)

            def link(ins):
                mark(ins)
                pool.wait_ge(pool_step, count[0])

            mark(G.memset(ident[:], 0.0))
            mark(G.memset(tri[:], 1.0))
            mark(G.memset(fill[:], 0.0))
            G.memset(neg_half[:], -0.5)
            mark(G.memset(pw[:, :, :, 0:1], 0.0))
            mark(G.memset(tab[:, :, 0:1], 0.0))
            G.memset(eps_c[:], EPS).then_inc(eps_ready, 1)
            for i in range(RING):
                G.memset(eights[:, i:i + 1], float(E ** i))
            mark(G.memset(tex_f[:], 0.0))
            G.memset(ones_b[:], 1.0)
            link(G.memset(ones_f, 1.0))
            G.affine_select(out=ident[:], in_=ident[:], compare_op=ALU.not_equal, fill=1.0,
                            base=0, pattern=[[1, P]], channel_multiplier=-1)
            G.affine_select(out=tri[:], in_=tri[:], compare_op=ALU.is_gt, fill=0.0,
                            base=0, pattern=[[1, P]], channel_multiplier=-1)
            G.iota(e_minus[:], pattern=[[1, E]], base=-E, channel_multiplier=0,
                   allow_small_or_imprecise_dtypes=True)
            G.iota(tile_at[:], pattern=[[P, NTILE]], base=0, channel_multiplier=0,
                   allow_small_or_imprecise_dtypes=True)
            G.iota(fill[:, :, D:RW].bitcast(I32), pattern=[[P, RING], [0, RW - D]],
                   base=NTOK, channel_multiplier=1).then_inc(fill_ready, 1)
            G.iota(xn[:, :, D:RW].bitcast(I32), pattern=[[P * CH, NB], [1, CH], [0, RW - D]],
                   base=0, channel_multiplier=CH).then_inc(const_ready, 1)

            mark(G.memset(pw[:, 1, :, 0:1], 1.0))
            mark(G.memset(tab[:, 1, 0:1], 1.0))

            for bb in range(2):
                n = slice(bb * CH, (bb + 1) * CH)
                pool.wait_ge(stat_ready, bb + 1)
                mark(G.tensor_scalar(std[:, n], mv[:, n, 1], EPS, None, ALU.add))
                link(G.tensor_scalar(nmr[:, n], mv[:, n, 0], -1.0, None, ALU.mult))
                link(G.tensor_tensor(rstd[:, n], std[:, n], neg_half[:], ALU.pow))
                G.tensor_tensor(nmr[:, n], nmr[:, n], rstd[:, n], ALU.mult).then_inc(rstd0_ready, 1)

            def normalise(bb):
                if bb >= 2:
                    pool.wait_ge(rstd_ready, bb // 2)
                for j in range(ACT_J, CH):
                    n = bb * CH + j
                    last = G.tensor_scalar(xn[:, n, 0:D], x_sb[:, bb, j, :], mv[:, n, 0:1], rstd[:, n:n + 1],
                                           ALU.subtract, ALU.mult)
                last.then_inc(xnp_ready, 1)

            def extend(powers, tmp, n):
                shape = list(powers[:, 1:3, ..., 0:n + 1].shape)
                re = powers[:, 1:2, ..., n:n + 1].broadcast_to(shape)
                im = powers[:, 2:3, ..., n:n + 1].broadcast_to(shape)
                a, b = tmp
                mark(G.tensor_tensor(a, powers[:, 1:3, ..., 0:n + 1], re, ALU.mult))
                link(G.tensor_tensor(b, powers[:, 0:2, ..., 0:n + 1], im, ALU.mult))
                link(G.tensor_tensor(powers[:, 1:3, ..., n:2 * n + 1], a, b, ALU.add))
                link(G.tensor_scalar(powers[:, 0, ..., n:2 * n + 1], powers[:, 2, ..., n:2 * n + 1], -1.0, None,
                                     ALU.mult))

            def extend_pw(n):
                extend(pw, [pwt[:, i, :, 0:2 * (n + 1)].rearrange("p a (c l) -> p a c l", c=2) for i in range(2)], n)

            pool.wait_ge(cs_ready, 1)
            link(G.tensor_scalar(pw[:, 1:3, 1, 1], pw[:, 1:3, 0, 1], mag[:, 0:1], None, ALU.mult))
            link(G.tensor_scalar(pw[:, 0, :, 1], pw[:, 2, :, 1], -1.0, None, ALU.mult))
            extend_pw(1)
            normalise(0)
            extend_pw(2)
            normalise(1)
            G.tensor_scalar(glam[:, :, :], pw[:, :, 1, :], pexp[:, 2:3], None, ALU.mult).then_inc(lam_ready, 1)
            normalise(2)
            pool.wait_ge(wT_ready, 1)
            for l in range(1, CH):
                G.tensor_scalar(tvp[:, l - 1, 0, :], wT[:, 1, :], pw[:, 2, 1, l:l + 1], None, ALU.mult)
                last = G.tensor_scalar(tvp[:, l - 1, 1, :], wT[:, 1, :], pw[:, 1, 1, l:l + 1], None, ALU.mult)
                if l == CH - 1:
                    last.then_inc(tvp_ready, 1)
                normalise(l + 2)
            for bb in range(CH + 2, NB):
                normalise(bb)
            pool.wait_ge(wmid_in, 16)
            G.tensor_scalar(gw[:, 0, :], wm[:, 0, :], pexp[:, 2:3], None, ALU.mult)
            mark(G.tensor_scalar(gw[:, 1, :], wm[:, 1, :], pexp[:, 2:3], -1.0, ALU.mult, ALU.mult))
            mark(G.tensor_scalar(lamt[:, 0, :, :], pw[:, 1:3, 1, 0:CH], bin_c[:, 0:1], None, ALU.mult))
            link(G.tensor_scalar(lamt[:, 1, :, :], pw[:, 0:2, 1, 0:CH], bin_c[:, 1:2], None, ALU.mult))
            mark(G.tensor_tensor(lamb[:, :, :], lamt[:, 0, :, :], lamt[:, 1, :, :], ALU.add))
            pool.wait_ge(pool_step, count[0])
            G.tensor_tensor(lamt[:, 0, :, 0:2], lamb[:, :, 0:2], lamb[:, :, 2:4], ALU.add).then_inc(gw_ready, 1)
            pool.wait_ge(gw_ready, 1)
            mark(G.tensor_tensor(vbias[:, 0:2], lamt[:, 0, :, 0], lamt[:, 0, :, 1], ALU.add))
            link(G.tensor_copy(tab[:, :, 1], pw[:, :, 0, CH]))
            n = 1
            while n < K:
                extend(tab, [tabt[:, i, :, 0:n + 1] for i in range(2)], n)
                n *= 2
            for hf in range(2):
                mark(G.memset(carry[hf].rearrange("p c (b k) -> p (c b) k", k=K)[:, :, 0:1], 0.0))
            pool.wait_ge(decay_ready, 1)
            mark(G.memset(bk(decay)[:, :, 0:1], 0.0))
            link(G.tensor_tensor(bm[:], bmid_c[:, 0:1], bmid_c[:, 1:2], ALU.subtract))
            G.tensor_tensor(bm[:], bm[:], bin_c[:, 2:3], ALU.add).then_inc(table_ready, 1)

            pool.wait_ge(filled, 16 * (RING + 1))
            pool.wait_ge(slot_ready, 1)
            for n in range(NT):
                G.indirect_dma_start(out=xs_dram, out_offset=bass.IndirectOffsetOnAxis(ap=slot[:, n:n + 1], axis=0),
                                     in_=xn[:, n, :], in_offset=None).then_inc(sorted_out, 16)

            def inverse_std(b, done):
                n = slice(b * HALF, (b + 1) * HALF)
                mark(G.tensor_scalar(fveps[:, n], fmv[:, n, 1], EPS, None, ALU.add))
                link(G.tensor_scalar(fnmean[:, n], fmv[:, n, 0], -1.0, None, ALU.mult))
                link(G.tensor_tensor(frstd[:, n], fveps[:, n], neg_half[:], ALU.pow))
                G.tensor_tensor(fnmr[:, n], fnmean[:, n], frstd[:, n], ALU.mult).then_inc(done, 1)

            def normalise_s(j):
                pool.wait_ge(frstd_ready, j + 1)
                for q in range(HALF):
                    n = j * HALF + q
                    mark(G.tensor_scalar(s_blk(j)[:, q, :], s_blk(j)[:, q, :], frstd[:, n:n + 1], fnmr[:, n:n + 1],
                                         ALU.mult, ALU.add))

            def affine(j, row, op):
                pool.wait_ge(pool_step, count[0])
                mark(G.tensor_tensor(s_blk(j), s_blk(j), row[:].unsqueeze(1).broadcast_to([P, HALF, D]), op))

            pool.wait_ge(row_ready, 2)
            for j in range(EARLY - 2):
                pool.wait_ge(fstat_ready, j + 1)
                inverse_std(j, frstd_ready)
            normalise_s(0)
            affine(0, g_row, ALU.mult)
            affine(0, b_row, ALU.add)
            for t in range(NTILE):
                pool.wait_ge(gate_ready, t + 1)
                G.indirect_dma_start(out=gate_dram, out_offset=bass.IndirectOffsetOnAxis(ap=token[:, t:t + 1], axis=0),
                                     in_=gate[:, t % RING, :], in_offset=None).then_inc(gate_out[t % RING], 16)
                if t < 2:
                    pool.wait_ge(fstat_ready, EARLY - 1 + t)
                    inverse_std(EARLY - 2 + t, frstd_ready)
                j, stage_of = divmod(t + 3, 5)
                if 0 < j < EARLY:
                    if stage_of == 0:
                        normalise_s(j)
                    elif stage_of == 2:
                        affine(j, g_row, ALU.mult)
                    elif stage_of == 4 and j < EARLY - 1:
                        affine(j, b_row, ALU.add)
                    elif stage_of == 4:
                        pool.wait_ge(pool_step, count[0])
                        G.tensor_tensor(s_blk(j), s_blk(j), b_row[:].unsqueeze(1).broadcast_to([P, HALF, D]),
                                        ALU.add).then_inc(early_ready, 1)

            def combine(bb):
                pool.wait_ge(gate_ld[bb], 16)
                link(G.tensor_tensor(s_sb[:, bb, :, :], s_sb[:, bb, :, :], gate_in[:, bb, :, :], ALU.mult))
                G.tensor_tensor(x_sb[:, bb, :, :], x_sb[:, bb, :, :], s_sb[:, bb, :, :],
                                ALU.add).then_inc(half0_ready, 1)

            pool.wait_ge(pool_step, count[0])
            combine(0)
            for bb in range(HALF, NB):
                pool.wait_ge(gate_ld[bb], 16)
            xk = x_sb[:, HALF:NB, EARLY - CH, :]
            link(G.tensor_tensor(q3(ra), gate_in[:, HALF:NB, EARLY - CH, :],
                                 b_row[:].unsqueeze(1).broadcast_to([P, HALF, D]), ALU.mult))
            G.tensor_tensor(xk, xk, q3(ra), ALU.add).then_inc(xbias_ready, 1)
            combine(2)
            pool.wait_ge(fstat_ready, EARLY + 1)
            inverse_std(EARLY, frstd_ready)
            pool.wait_ge(fstat_ready, EARLY + 2)
            inverse_std(EARLY + 1, frstd_ready)
            combine(3)

        @block.scalar
        def _(act):
            S = nc.scalar
            act.dma_start(cols_sb[:, :], columns).then_inc(par_in, 16)
            act.dma_start(w_small[:, 0:3, :], W_small[:, 0:3, :]).then_inc(win_in, 16)

            act.wait_ge(par_in, 16)
            S.activation(pexp[:], plog, ACT.Exp).then_inc(act_step, 1)
            act.wait_ge(act_step, 1)
            S.activation(mag[:, 0:1], pexp[:, 0:1], ACT.Exp, scale=-1.0)
            S.activation(mag[:, 1:2], pexp[:, 0:1], ACT.Exp, scale=-float(CH)).then_inc(exp_ready, 1)
            act.wait_ge(win_in, 32)
            S.copy(wg_h, wg[:]).then_inc(wgH_ready, 1)
            act.wait_ge(wT_done, 1)
            S.copy(wT[:, :, :], ps_wT[:, 0:2 * D]).then_inc(wT_ready, 1)

            act.wait_ge(ang_ready, 1)
            S.activation(pw[:, 1:3, 0, 1], ang[:, 4:6], ACT.Sin).then_inc(cs_ready, 1)

            def deviation(pair):
                act.wait_ge(stat_ready, 2 * pair + 2)
                n = slice(2 * pair * CH, 2 * (pair + 1) * CH)
                S.activation(std[:, n], mv[:, n, 1], ACT.Sqrt, bias=eps_c[:, 0:1]).then_inc(std_ready, 1)

            def normalise(bb):
                if bb < 2:
                    act.wait_ge(rstd0_ready, bb + 1)
                else:
                    act.wait_ge(rstd_ready, bb // 2)
                for j in range(ACT_J):
                    n = bb * CH + j
                    last = S.activation(xn[:, n, 0:D], x_sb[:, bb, j, :], ACT.Identity,
                                        bias=nmr[:, n:n + 1], scale=rstd[:, n:n + 1])
                last.then_inc(xn_ready, 1)

            def upper_x(bb):
                act.wait_ge(xT_done, bb + 1)
                S.copy(x_h[:, :, bb * P:(bb + 1) * P],
                       ps_x[bb % XB][:, :].rearrange("p (j c) -> p j c", j=CH)).then_inc(xH_ready, 1)

            act.wait_ge(eps_ready, 1)
            for bb in range(NB):
                normalise(bb)
                if bb % 2 and bb + 1 < NB:
                    deviation(bb // 2 + 1)
                if bb:
                    upper_x(bb - 1)
            upper_x(NB - 1)
            act.wait_ge(vT_done, 1)
            S.copy(v_h[:, 0, :, :], wi[:, 0:2, :])
            S.copy(v_h[:, 1:3, :, :], ps_vT[0][:, :])
            S.copy(v_h[:, 3, :, :], ps_vT[1][:, 0:2 * D]).then_inc(vH_ready, 1)
            act.wait_ge(lam_ready, 1)
            S.mul(decay, pw[:, 1, 1, 0:1].broadcast_to([P, COLS]), mag[:, 1:2]).then_inc(decay_ready, 1)
            act.wait_ge(row_in, 16 * 3)
            S.mul(g_row[:], g_row[:], 0.5).then_inc(row_ready, 1)
            S.mul(b_row[:], b_row[:], 0.5).then_inc(row_ready, 1)
            act.wait_ge(wmid_in, 16)
            for l in range(1, CH + 1):
                S.mul(wtmp[:, 0, l - 1, :], wm[:, 1, :], glam[:, 2, l:l + 1])
                last = S.mul(wtmp[:, 1, l - 1, :], wm[:, 1, :], glam[:, 1, l:l + 1])
            last.then_inc(wtmp_ready, 1)
            act.wait_ge(m0_ready, 1)
            S.copy(m_h[:, 0, :], m_0)
            S.copy(m_h[:, 1:CH, :], ps_m[:, D:CH * D]).then_inc(mH_ready, 1)

            def load_table(func):
                S.activation(unread[:], eps_c[:], func)

            def block_step(b, first, last):
                if b <= last:
                    act.wait_ge(o_done, b + 1)
                    if b >= 4:
                        act.wait_ge(y_ready, b - 3)
                    S.activation(outT[:, b % 4, :], ps_o[b % 2][:, :], ACT.Identity,
                                 bias=obias[:, b % CH:b % CH + 1]).then_inc(outT_ready, 1)
                k = b - 1
                if first <= k <= last:
                    act.wait_ge(w1_done, k + 1)
                    if k == 0:
                        act.wait_ge(bc_ready, CH)
                    if k >= 2:
                        act.wait_ge(w2_done, k - 1)
                    S.activation(g1[:, k % 2, :], ps_1[k % 2][:, :], ACT.Gelu,
                                 bias=w1b_c[:, 0:1]).then_inc(g1_ready, 1)
                    if k == EARLY - 1:
                        load_table(ACT.Gelu_apprx_tanh)
                k = b - 3
                if first <= k <= last:
                    act.wait_ge(yT_done, k + 1)
                    S.copy(s_blk(k), q3(ps_y[k % 2][:, :])).then_inc(ytok_ready, 1)

            def expert_weights(s, e):
                S.copy(up_t[:, s % 2, :], up_w[:, bass.ds(e, H)]).then_inc(upw_ready, 1)

            for b in range(EARLY + 1):
                block_step(b, 0, EARLY - 1)
                if b == 0:
                    act.wait_ge(bc_ready, CH)
                    S.copy(bc_h[:, :, :, :], bc_w[:, :, :, :]).then_inc(bcH_ready, 1)
                if b == 2:
                    for c in range(2):
                        act.wait_ge(carry_ready, 3 + c)
                        S.copy(carry_h[:, c, :], carry[1][:, c, :]).then_inc(carryH_ready, 1)
                if b == EARLY - 2:
                    act.wait_ge(tex_ready, 1)
                    act.wait_ge(up_in, 16)
                    e = experts(act, 0)
                    expert_weights(0, e[0])
                    expert_weights(1, e[1])

            def step(t, s, e):
                if s < NTILE:
                    act.wait_ge(up_done, t + 1)
                    if s >= RING:
                        act.wait_ge(down_done, t - RING + 1)
                    S.activation(hT[:, s % RING, :], ps_up[s % 2][:, :], ACT.Gelu_apprx_tanh).then_inc(hT_ready, 1)
                if s + 2 < NTILE:
                    expert_weights(s + 2, e)
                if s >= 2:
                    act.wait_ge(down_done, t - 1)
                    S.activation(th[:, s % 2, :], ps_dn[s % 2][:, 0:D], ACT.Tanh, scale=0.5).then_inc(th_ready, 1)

            block_step(EARLY + 1, 0, EARLY - 1)
            for t in range(HEAD):
                if t == 6:
                    e = experts(act, 2)
                step(t, t, e[t + 2 if t < 6 else t - 6])
                if t == 0:
                    block_step(EARLY + 2, 0, EARLY - 1)
            with act.Fori(0, ROUNDS) as i:
                e = experts(act, i + (HEAD + 2) // RING)
                for u in range(RING):
                    step(i * RING + HEAD + u, HEAD + u, e[u])
            t0 = HEAD + ROUNDS * RING
            e = experts(act, (t0 + 2) // RING)
            for t in range(t0, NTILE + 2):
                step(t, t, e[t - t0])

            load_table(ACT.Gelu)
            for b in range(EARLY, NBLK + 3):
                block_step(b, EARLY, NBLK - 1)
            act.wait_ge(frstd_ready, EARLY + 1)
            for q in range(HALF):
                n = EARLY * HALF + q
                last = S.activation(s_blk(EARLY)[:, q, :], s_blk(EARLY)[:, q, :], ACT.Identity,
                                    bias=fnmr[:, n:n + 1], scale=frstd[:, n:n + 1])
            last.then_inc(sn_ready, 1)
            for j in range(CH):
                act.wait_ge(half1_ready, j + 1)
                act.dma_start(out_dram[HALF:NB, :, j, :].rearrange("g p d -> p g d"),
                              x_sb[:, HALF:NB, j, :]).then_inc(stored, 16)

        @block.vector
        def _(dve):
            V = nc.vector
            count = [0]

            def mark(ins):
                count[0] += 1
                ins.then_inc(dve_step, 1)

            def settle():
                dve.wait_ge(dve_step, count[0])

            def link(ins):
                mark(ins)
                settle()

            def lower(dst, whole, upper):
                return V.tensor_tensor(dst, whole, upper.bitcast(F32), ALU.subtract)

            def stats(bb):
                dve.wait_ge(x_in[bb], 16)
                for j in range(CH):
                    mark(V.bn_stats(st[:, bb * CH + j, :], x_sb[:, bb, j, :]))
                settle()
                for j in range(CH):
                    last = V.bn_aggr(mv[:, bb * CH + j, :], st[:, bb * CH + j, :])
                last.then_inc(stat_ready, 1)

            def lower_x(bb):
                dve.wait_ge(xH_ready, bb + 1)
                lower(x_l[:, :, bb * P:(bb + 1) * P], ps_x[bb % XB][:, :].rearrange("p (j c) -> p j c", j=CH),
                      x_h[:, :, bb * P:(bb + 1) * P]).then_inc(xL_ready, 1)

            def inverse_std(pair):
                dve.wait_ge(std_ready, pair)
                n = slice(2 * pair * CH, 2 * (pair + 1) * CH)
                link(V.reciprocal(rstd[:, n], std[:, n]))
                V.scalar_tensor_tensor(out=nmr[:, n], in0=mv[:, n, 0], scalar=-1.0, in1=rstd[:, n],
                                       op0=ALU.mult, op1=ALU.mult).then_inc(rstd_ready, 1)

            stats(0)
            stats(1)
            dve.wait_ge(exp_ready, 1)
            link(V.tensor_scalar(angi[:], pexp[:, 1:2], 1.0 / TWO_PI, None, ALU.mult))
            link(V.tensor_copy(ang[:, 0:1], angi[:]))
            link(V.scalar_tensor_tensor(out=ang[:, 1:2], in0=ang[:, 0:1], scalar=-TWO_PI_HI, in1=pexp[:, 1:2],
                                        op0=ALU.mult, op1=ALU.add))
            link(V.scalar_tensor_tensor(out=ang[:, 2:3], in0=ang[:, 0:1], scalar=-TWO_PI_LO, in1=ang[:, 1:2],
                                        op0=ALU.mult, op1=ALU.add))
            link(V.tensor_scalar(ang[:, 5:6], ang[:, 2:3], 3.1415925, -3.1415925, ALU.min, ALU.max))
            link(V.scalar_tensor_tensor(out=ang[:, 3:4], in0=ang[:, 5:6], scalar=-1.0, in1=ang[:, 5:6],
                                        op0=ALU.mult, op1=ALU.max))
            V.tensor_scalar(ang[:, 4:5], ang[:, 3:4], -1.0, TWO_PI / 4, ALU.mult, ALU.add).then_inc(ang_ready, 1)
            stats(2)
            stats(3)
            dve.wait_ge(wgH_ready, 1)
            lower(wg_l, wg[:], wg_h).then_inc(wgL_ready, 1)
            stats(4)
            inverse_std(1)
            stats(5)
            lower_x(0)
            stats(6)
            lower_x(1)
            inverse_std(2)
            stats(7)
            lower_x(2)
            inverse_std(3)
            lower_x(3)
            dve.wait_ge(tvp_ready, 1)
            for l in range(1, CH):
                V.scalar_tensor_tensor(out=tv[:, l - 1, 0, :], in0=wT[:, 0, :], scalar=pw[:, 1, 1, l:l + 1],
                                       in1=tvp[:, l - 1, 0, :], op0=ALU.mult, op1=ALU.subtract)
                last = V.scalar_tensor_tensor(out=tv[:, l - 1, 1, :], in0=wT[:, 0, :], scalar=pw[:, 2, 1, l:l + 1],
                                              in1=tvp[:, l - 1, 1, :], op0=ALU.mult, op1=ALU.add)
            last.then_inc(tv_ready, 1)
            for bb in range(4, NB):
                lower_x(bb)

            dve.wait_ge(vH_ready, 1)
            lower(v_l[:, 0, :, :], wi[:, 0:2, :], v_h[:, 0, :, :])
            lower(v_l[:, 1:3, :, :], ps_vT[0][:, :], v_h[:, 1:3, :, :])
            lower(v_l[:, 3, :, :], ps_vT[1][:, 0:2 * D], v_h[:, 3, :, :]).then_inc(vL_ready, 1)

            dve.wait_ge(logits_done, 1)
            dve.wait_ge(row_in, 16 * 3)
            dve.wait_ge(const_ready, 1)
            parts = ps_lg[:, :].rearrange("p (n a e) -> p n a e", a=2, e=E)
            link(V.tensor_tensor(lg, parts[:, :, 0, :], bg_row[:].unsqueeze(1).broadcast_to([P, NT, E]), ALU.add))
            link(V.tensor_tensor(lg, lg, parts[:, :, 1, :], ALU.add))
            link(V.tensor_reduce(top[:], lg, AX_X, ALU.max))
            link(V.tensor_tensor(cand, lg, top[:].unsqueeze(2).broadcast_to([P, NT, E]), ALU.is_equal))
            link(V.tensor_tensor(cand, cand, e_minus[:].unsqueeze(1).broadcast_to([P, NT, E]), ALU.mult))
            link(V.tensor_reduce(pick[:], cand, AX_X, ALU.min))
            V.tensor_tensor(onehot, pick[:].unsqueeze(1).broadcast_to([P, E, NT]),
                            e_minus[:].unsqueeze(2).broadcast_to([P, E, NT]), ALU.is_equal).then_inc(onehot_ready, 1)
            dve.wait_ge(m_done, 1)
            V.tensor_tensor(m_0, ps_m[:, 0:D], wi[:, 2, :], ALU.add).then_inc(m0_ready, 1)
            dve.wait_ge(count_done, 1)
            before = ps_rt[:, 0:E * NT].rearrange("p (e n) -> p e n", e=E)
            link(V.tensor_copy(aug[:, :, 1:NT + 1], ps_rt[:, E * NT:2 * E * NT].rearrange("p (e n) -> p e n", e=E)))
            link(V.tensor_reduce(cnt[:], aug[:, :, 1:NT + 1], AX_X, ALU.add))
            link(V.tensor_scalar(cnti[:], cnt[:], float(P - 1), None, ALU.add))
            link(V.tensor_scalar(cnti[:], cnti[:], 7, 7, ALU.logical_shift_right, ALU.logical_shift_left))
            mark(V.memset(aug[:, 0, 0:1], 0.0))
            link(V.tensor_tensor(aug[:, 1:E, 0], cnti[:, 0:E - 1], cnt[:, 0:E - 1], ALU.subtract))
            link(V.tensor_tensor_scan(base.rearrange("p e n -> p (e n)"), ones_f,
                                      aug.rearrange("p e n -> p (e n)"), 0.0, ALU.mult, ALU.add))
            link(V.tensor_tensor(posm, before, base[:, :, 0:NT], ALU.add))
            link(V.tensor_tensor(posm, posm, onehot, ALU.mult))
            link(V.tensor_reduce(slot_f[:], posm.rearrange("p e n -> p n e"), AX_X, ALU.add))
            V.tensor_copy(slot[:], slot_f[:]).then_inc(slot_ready, 1)
            def rotate(hf):
                vr, vi = ps_v[hf]
                br, bi = vbias[:, 0:1], vbias[:, 1:2]
                dve.wait_ge(vin_done, 2 * hf + 2)
                if hf:
                    dve.wait_ge(carry_ready, 2 * hf)
                for dst, src, b, tb in ((ra, vr, br, cosk), (rb, vi, bi, sink), (rc, vi, bi, cosk), (rd, vr, br, sink)):
                    last = V.scalar_tensor_tensor(out=bk(dst), in0=bk(src[:]), scalar=b, in1=over_b(tb),
                                                  op0=ALU.add, op1=ALU.mult)
                last.then_inc(rot_ready, 1)

            def scan(hf):
                dve.wait_ge(rot_ready, hf + 1)
                mark(V.tensor_tensor(ra, ra, rb, ALU.add))
                link(V.tensor_tensor(rc, rc, rd, ALU.subtract))
                mark(V.tensor_tensor_scan(rb, decay, ra, 0.0, ALU.mult, ALU.add))
                mark(V.tensor_tensor_scan(rd, decay, rc, 0.0, ALU.mult, ALU.add))

            def rotate_back_products(hf, c):
                tab_r, tab_i = ((cosk, sink), (sink, cosk))[c]
                settle()
                if c:
                    dve.wait_ge(carry_ready, 2 * hf + 1)
                mark(V.tensor_tensor(bk(ra), bk(rb), over_b(tab_r), ALU.mult))
                mark(V.tensor_tensor(bk(rc), bk(rd), over_b(tab_i), ALU.mult))

            def rotate_back_sum(hf, c):
                settle()
                V.tensor_tensor(bk(carry[hf][:, c, :])[:, :, 1:K], bk(ra)[:, :, 0:K - 1],
                                bk(rc)[:, :, 0:K - 1], (ALU.subtract, ALU.add)[c]).then_inc(carry_ready, 1)

            def rotate_back(hf, c):
                rotate_back_products(hf, c)
                rotate_back_sum(hf, c)

            dve.wait_ge(table_ready, 1)
            dve.wait_ge(mH_ready, 1)
            dve.wait_ge(m0_ready, 1)
            lower(m_l[:, 0, :], m_0, m_h[:, 0, :])
            lower(m_l[:, 1:CH, :], ps_m[:, D:CH * D], m_h[:, 1:CH, :])
            V.tensor_tensor_scan(obias[:], pw[:, 1, 1, 0:1].broadcast_to([P, CH]), ps_mb[:, 0:CH], bm[:, 0:1],
                                 ALU.mult, ALU.add).then_inc(mL_ready, 1)
            rotate(0)
            def carry_weights(l):
                dve.wait_ge(wtmp_ready, 1)
                V.scalar_tensor_tensor(out=b_w[:, l - 1, :], in0=wm[:, 0, :], scalar=glam[:, 1, l:l + 1],
                                       in1=wtmp[:, 0, l - 1, :], op0=ALU.mult, op1=ALU.subtract)
                V.scalar_tensor_tensor(out=c_w[:, l - 1, :], in0=wm[:, 0, :], scalar=glam[:, 0, l:l + 1],
                                       in1=wtmp[:, 1, l - 1, :], op0=ALU.mult, op1=ALU.subtract).then_inc(bc_ready, 1)

            scan(0)
            rotate_back(0, 0)
            rotate_back(0, 1)
            for l in range(1, CH + 1):
                carry_weights(l)
            rotate(1)
            scan(1)

            def block_sum(k):
                dve.wait_ge(w2_done, k + 1)
                if k >= 2:
                    dve.wait_ge(yT_done, k - 1)
                V.scalar_tensor_tensor(out=yT[:, k % 2, :], in0=ps_2[k % 2][:, :], scalar=w2b_c[:, 0:1],
                                       in1=outT[:, k % 4, :], op0=ALU.add, op1=ALU.add).then_inc(y_ready, 1)

            def block_stats(k):
                dve.wait_ge(ytok_ready, k + 1)
                for q in range(HALF):
                    mark(V.bn_stats(fst[:, k * HALF + q, :], s_blk(k)[:, q, :]))
                settle()
                for q in range(HALF):
                    fin = V.bn_aggr(fmv[:, k * HALF + q, :], fst[:, k * HALF + q, :])
                fin.then_inc(fstat_ready, 1)

            def block_step(b, first, last):
                if first <= b - 2 <= last:
                    block_sum(b - 2)
                if first <= b - 3 <= last:
                    block_stats(b - 3)

            dve.wait_ge(bcH_ready, 1)
            lower(bc_l[:, :, :, :], bc_w[:, :, :, :], bc_h[:, :, :, :]).then_inc(bcL_ready, 1)
            rotate_back(1, 0)
            rotate_back(1, 1)
            block_step(2, 0, EARLY - 1)
            for c in range(2):
                dve.wait_ge(carryH_ready, c + 1)
                lower(carry_l[:, c, :], carry[1][:, c, :], carry_h[:, c, :]).then_inc(carryL_ready, 1)
            dve.wait_ge(filled, 16 * (RING + 1))
            link(V.tensor_tensor(tcmp, tile_at[:].unsqueeze(2).broadcast_to([P, NTILE, E - 1]),
                                 base[:, 1:E, 0].unsqueeze(1).broadcast_to([P, NTILE, E - 1]), ALU.is_ge))
            dve.wait_ge(const_ready, 1)
            link(V.tensor_reduce(tex_f[:].rearrange("p m i -> p (m i)")[:, 0:NTILE], tcmp, AX_X, ALU.add))
            link(V.tensor_tensor(tex_f[:], tex_f[:], eights[:].unsqueeze(1).broadcast_to([P, NWORD + 1, RING]),
                                 ALU.mult))
            link(V.tensor_reduce(tex_r[:], tex_f[:], AX_X, ALU.add))
            V.scalar_tensor_tensor(out=tex[:], in0=tex_r[:, 1:NWORD + 1, 0], scalar=float(E ** RING),
                                   in1=tex_r[:, 0:NWORD, 0], op0=ALU.mult, op1=ALU.add).then_inc(tex_ready, 1)
            for b in range(3, EARLY):
                block_step(b, 0, EARLY - 1)

            def copy_xs(t, s):
                dve.wait_ge(xsT_done, t + 1)
                V.tensor_copy(token[:, bass.ds(t, 1)], xs_in[:, s % RING, D:D + 1].bitcast(I32))
                V.tensor_copy(xsT[:, s % 2, :], ps_xs[s % 2][:, 0:P]).then_inc(xsT_ready, 1)

            def silu2(t, s, rnd):
                dve.wait_ge(th_ready, t + 1)
                if s >= RING:
                    dve.wait_ge(gate_out[s % RING], rnd * 16)
                V.scalar_tensor_tensor(out=gate[:, s % RING, :], in0=th[:, s % 2, :], scalar=1.0,
                                       in1=ps_dn[s % 2][:, 0:D], op0=ALU.add, op1=ALU.mult).then_inc(gate_ready, 1)

            def step(t, s, rnd):
                if s + 1 < NTILE:
                    copy_xs(t + 1, s + 1)
                if s >= 2:
                    silu2(t - 2, s - 2, rnd)

            block_sum(EARLY - 2)
            copy_xs(0, 0)
            block_sum(EARLY - 1)
            for t in range(HEAD):
                step(t, t, (t - 2) // RING)
                if t < 3:
                    block_stats(EARLY - 3 + t)
            with dve.Fori(0, ROUNDS) as i:
                for u in range(RING):
                    step(i * RING + HEAD + u, HEAD + u, i + (HEAD + u - 2) // RING)
            for t in range(HEAD + ROUNDS * RING, NTILE + 2):
                step(t, t, (t - 2) // RING)

            def gated_sum(xk, y, gates, done):
                settle()
                link(V.tensor_tensor(y, y, gates, ALU.mult))
                V.tensor_tensor(xk, xk, y, ALU.add).then_inc(done, 1)

            def combine(k):
                gated_sum(x_sb[:, HALF:NB, k - CH, :], s_blk(k), gate_in[:, HALF:NB, k - CH, :], half1_ready)

            dve.wait_ge(early_ready, 1)
            dve.wait_ge(gate_ld[1], 16)
            gated_sum(x_sb[:, 1, :, :], s_sb[:, 1, :, :], gate_in[:, 1, :, :], group1_ready)
            for bb in range(HALF, NB):
                dve.wait_ge(gate_ld[bb], 16)
            combine(CH)
            dve.wait_ge(row_ready, 2)
            block_sum(EARLY)
            block_sum(EARLY + 1)
            mark(V.tensor_tensor(q3(rb), gate_in[:, HALF:NB, EARLY - CH, :],
                                 g_row[:].unsqueeze(1).broadcast_to([P, HALF, D]), ALU.mult))
            block_stats(EARLY)
            block_stats(EARLY + 1)
            y, n0 = s_blk(NBLK - 1), (NBLK - 1) * HALF
            dve.wait_ge(fstat_ready, NBLK)
            for q in range(HALF):
                mark(V.scalar_tensor_tensor(out=y[:, q, :], in0=y[:, q, :], scalar=fmv[:, n0 + q, 0:1],
                                            in1=g_row[:], op0=ALU.subtract, op1=ALU.mult))
            for k in range(CH + 1, EARLY):
                combine(k)
            dve.wait_ge(sn_ready, 1)
            y_prev, x_prev = s_blk(EARLY), x_sb[:, HALF:NB, EARLY - CH, :]
            link(V.tensor_tensor(y_prev, y_prev, q3(rb), ALU.mult))
            dve.wait_ge(xbias_ready, 1)
            V.tensor_tensor(x_prev, x_prev, y_prev, ALU.add).then_inc(half1_ready, 1)
            dve.wait_ge(frstd_ready, NBLK)
            for q in range(HALF):
                mark(V.scalar_tensor_tensor(out=y[:, q, :], in0=y[:, q, :], scalar=frstd[:, n0 + q:n0 + q + 1],
                                            in1=b_row[:], op0=ALU.mult, op1=ALU.add))
            combine(NBLK - 1)

        @block.tensor
        def _(pe):
            mm, tr = nc.tensor.matmul, nc.tensor.transpose

            def mm3(dst, a_h, a_l, b_h, b_l, start, stop):
                mm(dst, a_h, b_h, start=start, stop=False)
                mm(dst, a_h, b_l, start=False, stop=False)
                return mm(dst, a_l, b_h, start=False, stop=stop)

            pe.wait_ge(const_ready, 1)
            pe.wait_ge(win_in, 16 * 2)
            tr(ps_wT[:, 0:D], wi[:, 0, :], ident[:])
            tr(ps_wT[:, D:2 * D], wi[:, 1, :], ident[:]).then_inc(wT_done, 1)

            def logits(bb):
                pe.wait_ge(xL_ready, bb + 1)
                for j in range(CH):
                    n = bb * CH + j
                    tok = slice(bb * P, (bb + 1) * P)
                    dst = ps_lg[:, 2 * n * E:2 * (n + 1) * E]
                    mm(dst, x_h[:, j, tok], wg_hl[:, :], start=True, stop=False)
                    last = mm(dst[:, 0:E], x_l[:, j, tok], wg_h, start=False, stop=True)
                return last

            def busy(n, dst):
                for _ in range(n):
                    mm(dst[:, 0:P], ones_b[:], ones_b[:], start=True, stop=True)

            pe.wait_ge(wgL_ready, 1)
            for bb in range(NB):
                busy(WARM_FIRST if bb == 0 else WARM, ps_rt)
                pe.wait_ge(xn_ready, bb + 1)
                pe.wait_ge(xnp_ready, bb + 1)
                if bb >= XB:
                    pe.wait_ge(xL_ready, bb - XB + 1)
                for j in range(CH):
                    last = tr(ps_x[bb % XB][:, j * P:(j + 1) * P], xn[:, bb * CH + j, 0:D], ident[:])
                last.then_inc(xT_done, 1)
                if bb == NB - 1:
                    pe.wait_ge(tv_ready, 1)
                    for i in range(2 * (CH - 1)):
                        l, c = divmod(i, 2)
                        v = tr(ps_vT[i // 4][:, (i % 4) * D:(i % 4 + 1) * D], tv[:, l, c, :], ident[:])
                    v.then_inc(vT_done, 1)
                if bb >= 3:
                    logits(bb - 3)
            logits(NB - 3)
            logits(NB - 2)
            logits(NB - 1).then_inc(logits_done, 1)

            pe.wait_ge(vL_ready, 1)
            def chunk_sums(hf, c, steps=range(CH)):
                cols = slice(hf * COLS, (hf + 1) * COLS)
                for i in steps:
                    l = CH - 1 - i
                    last = mm3(ps_v[hf][c][:, :], v_h[:, l, c, :], v_l[:, l, c, :], x_h[:, i, cols], x_l[:, i, cols],
                               start=(i == 0), stop=(i == CH - 1))
                if i == CH - 1:
                    last.then_inc(vin_done, 1)

            chunk_sums(0, 0, range(FIRST))
            pe.wait_ge(gw_ready, 1)
            for l in range(CH):
                w = wT[:, :, :] if l == 0 else tv[:, l - 1, :, :]
                mm(ps_m[:, l * D:(l + 1) * D], w[:, 0, :], gw[:, 0, :], start=True, stop=False)
                mm(ps_m[:, l * D:(l + 1) * D], w[:, 1, :], gw[:, 1, :], start=False, stop=True)
            mm(ps_mb[:, 0:CH], gw[:, 0, :], lamb[:, 0, :], start=True, stop=False)
            mm(ps_mb[:, 0:CH], gw[:, 1, :], lamb[:, 1, :], start=False, stop=True).then_inc(m_done, 1)
            pe.wait_ge(onehot_ready, 1)
            hot = onehot.rearrange("p e n -> p (e n)")
            mm(ps_rt[:, 0:E * NT], tri[:], hot, start=True, stop=True)
            mm(ps_rt[:, E * NT:2 * E * NT], ones_b[:], hot, start=True, stop=True).then_inc(count_done, 1)
            chunk_sums(0, 0, range(FIRST, CH))
            chunk_sums(0, 1)
            chunk_sums(1, 0)
            chunk_sums(1, 1)
            pe.wait_ge(mL_ready, 1)

            def inputs(b):
                hf, j = divmod(b, CH)
                cols = slice(hf * COLS, (hf + 1) * COLS)
                if b >= 2:
                    pe.wait_ge(outT_ready, b - 1)
                if b == EARLY:
                    pe.wait_ge(xsT_ready, NTILE)
                elif b == EARLY + 1:
                    pe.wait_ge(hT_ready, NTILE)
                for i in range(j + 1):
                    mm3(ps_o[b % 2][:, :], m_h[:, j - i, :], m_l[:, j - i, :], x_h[:, i, cols], x_l[:, i, cols],
                        start=(i == 0), stop=False)

            def carried(b):
                hf, j = divmod(b, CH)
                cols = slice(hf * COLS, (hf + 1) * COLS)
                if hf == 0:
                    pe.wait_ge(carry_ready, 2)
                    pe.wait_ge(bc_ready, j + 1)
                    for c in range(2):
                        last = mm(ps_o[b % 2][:, :], bc_w[:, c, j, :], carry[0][:, c, :], start=False, stop=(c == 1))
                else:
                    pe.wait_ge(bcL_ready, 1)
                    for c in range(2):
                        pe.wait_ge(carryL_ready, c + 1)
                        last = mm3(ps_o[b % 2][:, :], bc_h[:, c, j, :], bc_l[:, c, j, :], carry_h[:, c, :],
                                   carry_l[:, c, :], start=False, stop=(c == 1))
                last.then_inc(o_done, 1)

            def block_step(b, first, last):
                if b <= last:
                    if b == 0:
                        inputs(0)
                        inputs(1)
                        busy(WARM_CARRY, ps_lg)
                    elif b >= 2:
                        inputs(b)
                    carried(b)
                k = b - 1
                if first <= k <= last:
                    pe.wait_ge(outT_ready, k + 1)
                    mm(ps_1[k % 2][:, :], w1s, outT[:, k % 4, :], start=True, stop=True).then_inc(w1_done, 1)
                k = b - 2
                if first <= k <= last:
                    pe.wait_ge(g1_ready, k + 1)
                    if k == 0:
                        pe.wait_ge(rot_ready, 2)
                    if k >= 2:
                        pe.wait_ge(y_ready, k - 1)
                    mm(ps_2[k % 2][:, :], w2s, g1[:, k % 2, :], start=True, stop=True).then_inc(w2_done, 1)
                k = b - 3
                if first <= k <= last:
                    pe.wait_ge(y_ready, k + 1)
                    if k >= 2:
                        pe.wait_ge(ytok_ready, k - 1)
                    if k == EARLY:
                        pe.wait_ge(gate_ready, NTILE)
                    for q in range(HALF):
                        fin = tr(ps_y[k % 2][:, q * P:(q + 1) * P], yT[:, k % 2, q * P:(q + 1) * P], ident[:])
                    fin.then_inc(yT_done, 1)

            for b in range(EARLY):
                block_step(b, 0, EARLY - 1)


            def transpose_x(t, s, rnd):
                r = s % RING
                pe.wait_ge(xs_ld[r], rnd * 16 + 16)
                tr(ps_xs[s % 2][:, 0:P], xs_in[:, r, 0:D], ident[:]).then_inc(xsT_done, 1)

            def up(t, s):
                pe.wait_ge(xsT_ready, t + 1)
                pe.wait_ge(upw_ready, t + 1)
                if s >= 2:
                    pe.wait_ge(hT_ready, t - 1)
                for c in range(HC):
                    last = mm(ps_up[s % 2][:, c * P:(c + 1) * P], up_t[:, s % 2, c * P:(c + 1) * P], xsT[:, s % 2, :],
                              start=True, stop=True)
                last.then_inc(up_done, 1)

            def down(t, s, e):
                dst = ps_dn[s % 2][:, 0:D]
                pe.wait_ge(hT_ready, t + 1)
                if s >= 2:
                    pe.wait_ge(gate_ready, t - 1)
                for c in range(HC):
                    last = mm(dst, hT[:, s % RING, c * P:(c + 1) * P], down_w[:, bass.ds(e + c * D, D)],
                              start=(c == 0), stop=(c == HC - 1))
                last.then_inc(down_done, 1)

            def first_part(t, s, rnd):
                if s + 1 < NTILE:
                    transpose_x(t + 1, s + 1, rnd)
                if s < NTILE:
                    up(t, s)

            def steps(t0, s0, n, e, rnd_of, between=None):
                lo = RING * ((s0 - 2) // RING) if s0 else 0
                for u in range(n):
                    s = s0 + u
                    if between:
                        between(s)
                    if s >= 2:
                        down(t0 + u - 2, s - 2, e[s - 2 - lo])
                    first_part(t0 + u + 1, s + 1, rnd_of(u))

            def head(s):
                if s == 0:
                    block_step(EARLY + 2, 0, EARLY - 1)
                elif s == 2:
                    pe.wait_ge(down_in, 16)
                    pe.wait_ge(ytok_ready, EARLY)

            pe.wait_ge(tex_ready, 1)
            e = experts(pe, 0)
            block_step(EARLY, 0, EARLY - 1)
            pe.wait_ge(outT_ready, EARLY)
            transpose_x(0, 0, 0)
            block_step(EARLY + 1, 0, EARLY - 1)
            pe.wait_ge(g1_ready, EARLY)
            first_part(0, 0, 0)
            steps(0, 0, 6, e, lambda u: (u + 2) // RING, head)
            steps(6, 6, RING, experts(pe, 1), lambda u: (u + 8) // RING)
            with pe.Fori(0, ROUNDS) as i:
                steps(i * RING + HEAD, HEAD, RING, experts(pe, i + (HEAD - 2) // RING),
                      lambda u: i + (HEAD + u + 2) // RING)
            t = HEAD + ROUNDS * RING
            steps(t, t, NTILE + 2 - t, experts(pe, (t - 2) // RING), lambda u: (t + u + 2) // RING)

            for b in range(EARLY, NBLK + 3):
                block_step(b, EARLY, NBLK - 1)


def kernel(L0_attn_x, L0_attn_W_in, L0_attn_b_in, L0_attn_params_log, L0_attn_W_mid, L0_attn_b_mid,
           L0_attn_w1_w, L0_attn_w1_b, L0_attn_w2_w, L0_attn_w2_b, L0_attn_ln_g, L0_attn_ln_b,
           L0_ffn_W1, L0_ffn_W2, L0_ffn_Wg, L0_ffn_bg):
    import numpy as np
    import concourse.bacc as bacc
    from concourse.bass_utils import run_bass_kernel_spmd

    E, H, D = L0_ffn_W2.shape
    laid_out = {
        "x": L0_attn_x,
        "w_small": np.concatenate([L0_attn_W_in, L0_attn_W_mid, L0_attn_w1_w[None], L0_attn_w2_w[None]]
                                  ).transpose(1, 0, 2),
        "columns": np.concatenate([L0_attn_params_log, L0_attn_b_in, L0_attn_b_mid, L0_attn_w1_b[None],
                                   L0_attn_w2_b[None]]).transpose(1, 0),
        "rows": np.stack([L0_attn_ln_g, L0_attn_ln_b]),
        "w1": np.asarray(L0_ffn_W1).transpose(1, 0, 2),
        "w2": np.asarray(L0_ffn_W2).reshape(E, H // P, P, D).transpose(2, 0, 1, 3),
        "wg": L0_ffn_Wg,
        "bg": L0_ffn_bg,
    }
    nc = bacc.Bacc("TRN2", target_bir_lowering=False, num_devices=1)
    arrays, args = {}, []
    for name, value in laid_out.items():
        a = np.ascontiguousarray(value)
        arrays[f"{name}_dram"] = a
        args.append(nc.dram_tensor(f"{name}_dram", a.shape, mybir.dt.from_np(a.dtype), kind="ExternalInput").ap())
    out = nc.dram_tensor("out_dram", L0_attn_x.shape, F32, kind="ExternalOutput").ap()
    lru_moe(nc, *args, out)
    r = run_bass_kernel_spmd(nc, [arrays], core_ids=[0])
    return r.results[0]["out_dram"]
```
